# Optimizing a Trainium2 kernel written in Bass

```python
import numpy as np
import jax
import jax.numpy as jnp

def _softmax(x, axis=-1):
    return jax.nn.softmax(x, axis=axis)

def _gelu(x):
    return jax.nn.gelu(x, approximate=True)

def _silu(x):
    return jax.nn.silu(x)

def _sigmoid(x):
    return jax.nn.sigmoid(x)

def _layernorm(x, axis=-1, eps=1e-05):
    m = jnp.mean(x, axis=axis, keepdims=True)
    v = jnp.var(x, axis=axis, keepdims=True)
    return (x - m) / jnp.sqrt(v + eps)

def _scatter_add(tgt, idx, src, axis=0):
    return tgt.at[idx].add(src)

def _segment_sum(src, seg, n):
    return jax.ops.segment_sum(src, seg, n)
kernel_name = 'mk_xattn_ffn_d1_seqx_r8_c8a8ea'

def setup_inputs(seed: int=0):
    np.random.seed(seed)
    _w = jnp.asarray

    def _rec_inputs():
        import jax
        import jax.numpy as jnp
        _rk = jax.random.key(seed)
        x = 7.22e-05 + 1 * jax.random.normal(jax.random.fold_in(_rk, 1), (4, 256, 256), jnp.float32)
        _lenS = 256 - jax.random.randint(jax.random.fold_in(_rk, 7), (4,), 0, max(1, 256 // 4) + 1, jnp.int32)
        _lenS2 = 256 - jax.random.randint(jax.random.fold_in(_rk, 8), (4,), 0, max(1, 256 // 4) + 1, jnp.int32)
        _ctx_1024P = jax.random.normal(jax.random.fold_in(_rk, 11), (4, 16, 128), jnp.float32)
        _ctx_1024c = jax.random.dirichlet(jax.random.fold_in(_rk, 511), 0.3 * jnp.ones((16,), jnp.float32), (4, 256))
        _ctx_1024t = jnp.einsum('bsk,bkd->bsd', _ctx_1024c, _ctx_1024P)
        _ctx_1024t = _ctx_1024t * jax.lax.rsqrt(jnp.mean(jnp.square(_ctx_1024t)) + 1e-12) * 0.953939
        ctx_1024 = -1.39393e-06 + 0.999914 * (_ctx_1024t + 0.3 * jax.random.normal(jax.random.fold_in(_rk, 611), (4, 256, 128), jnp.float32))
        fside_BxSx2_0 = jax.random.uniform(jax.random.fold_in(_rk, 12), (4, 256, 2), jnp.float32, 0.0, 0.999707)
        return (x, ctx_1024, fside_BxSx2_0)
    x, ctx_1024, fside_BxSx2_0 = _rec_inputs()

    def _L0_xattn_setup():
        import jax, jax.numpy as jnp
        import numpy as np
        DIM = 256
        CTX_DIM = 128
        N_HEADS = 32
        HEAD_DIM = DIM // N_HEADS
        POS_DIM = 2
        B, N, CTXN = (2, 256, 256)
        ROPE_BASE = 10000.0

        def apply_axial_rope(x, pos):
            b, n, h, d = x.shape
            p = pos.shape[-1]
            dpa = d // p
            half = dpa // 2
            freqs = ROPE_BASE ** (-jnp.arange(half, dtype=x.dtype) / half)
            ang = pos[..., :, None] * freqs
            cos = jnp.cos(ang)[:, :, None, :, :]
            sin = jnp.sin(ang)[:, :, None, :, :]
            xr = x.reshape(b, n, h, p, half, 2)
            x1, x2 = (xr[..., 0], xr[..., 1])
            out = jnp.stack([x1 * cos - x2 * sin, x1 * sin + x2 * cos], axis=-1)
            return out.reshape(b, n, h, d)
        key = jax.random.key(seed)
        ks = jax.random.split(key, 8)
        x = jax.random.normal(ks[0], (B, N, DIM), jnp.float32)
        ctx = jax.random.normal(ks[1], (B, CTXN, CTX_DIM), jnp.float32)
        pos_map = jax.random.uniform(ks[2], (B, N, POS_DIM), jnp.float32)
        ctx_pos_map = jax.random.uniform(ks[3], (B, CTXN, POS_DIM), jnp.float32)
        Wq = jax.random.normal(ks[4], (DIM, DIM), jnp.float32) / np.sqrt(DIM)
        Wkv = jax.random.normal(ks[5], (CTX_DIM, 2 * DIM), jnp.float32) / np.sqrt(CTX_DIM)
        Wout = jax.random.normal(ks[6], (DIM, DIM), jnp.float32) / np.sqrt(DIM)
        bout = jnp.zeros((DIM,), jnp.float32)
        return {'x': x, 'ctx': ctx, 'pos_map': pos_map, 'ctx_pos_map': ctx_pos_map, 'Wq': Wq, 'Wkv': Wkv, 'Wout': Wout, 'bout': bout}
    _L0_xattn_all = _L0_xattn_setup()
    _L0_xattn_in = {k: v for k, v in _L0_xattn_all.items() if k in ('Wq', 'Wkv', 'Wout', 'bout')}
    del _L0_xattn_all

    def _L0_ffn_setup():
        import jax, jax.numpy as jnp
        import numpy as np
        HID = 256
        INTER = 1024
        NEXP = 8
        TOPK = 2
        EPS = 1e-05

        def _mock_fused_moe(x, selected_experts, routing_weights, expert_weight):
            y = jnp.einsum('bsh,hd->bsd', x, expert_weight)
            scale = routing_weights.sum(axis=-1, keepdims=True)
            return y * scale
        key = jax.random.key(seed)
        ks = jax.random.split(key, 6)
        s = lambda fan_in: 1.0 / np.sqrt(fan_in)
        return {'hidden_states': jax.random.normal(ks[0], (4, 512, HID), dtype=jnp.float32), 'gate_w': jax.random.uniform(ks[1], (HID, NEXP), jnp.float32, -s(HID), s(HID)), 'up_w': jax.random.uniform(ks[2], (HID, INTER), jnp.float32, -s(HID), s(HID)), 'down_w': jax.random.uniform(ks[3], (INTER, HID), jnp.float32, -s(INTER), s(INTER)), 'expert_weight': jax.random.normal(ks[4], (HID, HID), dtype=jnp.float32), 'ln_gamma': jnp.ones((HID,), jnp.float32), 'ln_beta': jnp.zeros((HID,), jnp.float32)}
    _L0_ffn_all = _L0_ffn_setup()
    _L0_ffn_in = {k: v for k, v in _L0_ffn_all.items() if k in ('gate_w', 'up_w', 'down_w', 'expert_weight', 'ln_gamma', 'ln_beta')}
    del _L0_ffn_all
    return {'x': x, 'ctx_1024': ctx_1024, 'fside_BxSx2_0': fside_BxSx2_0, 'L0_xattn_Wq': _L0_xattn_in['Wq'], 'L0_xattn_Wkv': _L0_xattn_in['Wkv'], 'L0_xattn_Wout': _L0_xattn_in['Wout'], 'L0_xattn_bout': _L0_xattn_in['bout'], 'L0_ffn_gate_w': _L0_ffn_in['gate_w'], 'L0_ffn_up_w': _L0_ffn_in['up_w'], 'L0_ffn_down_w': _L0_ffn_in['down_w'], 'L0_ffn_expert_weight': _L0_ffn_in['expert_weight'], 'L0_ffn_ln_gamma': _L0_ffn_in['ln_gamma'], 'L0_ffn_ln_beta': _L0_ffn_in['ln_beta']}

def reference(x, ctx_1024, fside_BxSx2_0, L0_xattn_Wq, L0_xattn_Wkv, L0_xattn_Wout, L0_xattn_bout, L0_ffn_gate_w, L0_ffn_up_w, L0_ffn_down_w, L0_ffn_expert_weight, L0_ffn_ln_gamma, L0_ffn_ln_beta):
    import jax
    import jax.numpy as jnp

    def _L0_xattn_ref(x, ctx, pos_map, ctx_pos_map, Wq, Wkv, Wout, bout):
        import jax, jax.numpy as jnp
        import numpy as np
        DIM = 256
        CTX_DIM = 128
        N_HEADS = 32
        HEAD_DIM = DIM // N_HEADS
        POS_DIM = 2
        B, N, CTXN = (2, 256, 256)
        ROPE_BASE = 10000.0

        def apply_axial_rope(x, pos):
            b, n, h, d = x.shape
            p = pos.shape[-1]
            dpa = d // p
            half = dpa // 2
            freqs = ROPE_BASE ** (-jnp.arange(half, dtype=x.dtype) / half)
            ang = pos[..., :, None] * freqs
            cos = jnp.cos(ang)[:, :, None, :, :]
            sin = jnp.sin(ang)[:, :, None, :, :]
            xr = x.reshape(b, n, h, p, half, 2)
            x1, x2 = (xr[..., 0], xr[..., 1])
            out = jnp.stack([x1 * cos - x2 * sin, x1 * sin + x2 * cos], axis=-1)
            return out.reshape(b, n, h, d)
        b, n, _ = x.shape
        ctx_n = ctx.shape[1]
        q = (x @ Wq).reshape(b, n, N_HEADS, HEAD_DIM)
        k, v = jnp.split(ctx @ Wkv, 2, axis=-1)
        k = k.reshape(b, ctx_n, N_HEADS, HEAD_DIM)
        v = v.reshape(b, ctx_n, N_HEADS, HEAD_DIM)
        q = apply_axial_rope(q, pos_map)
        k = apply_axial_rope(k, ctx_pos_map)
        scale = 1.0 / np.sqrt(HEAD_DIM).astype(np.float32)
        logits = jnp.einsum('bqhd,bkhd->bhqk', q, k) * scale
        w = jax.nn.softmax(logits, axis=-1)
        attn = jnp.einsum('bhqk,bkhd->bqhd', w, v)
        attn = attn.reshape(b, n, N_HEADS * HEAD_DIM)
        return attn @ Wout + bout

    def _L0_ffn_ref(hidden_states, gate_w, up_w, down_w, expert_weight, ln_gamma, ln_beta):
        import jax, jax.numpy as jnp
        import numpy as np
        HID = 256
        INTER = 1024
        NEXP = 8
        TOPK = 2
        EPS = 1e-05

        def _mock_fused_moe(x, selected_experts, routing_weights, expert_weight):
            y = jnp.einsum('bsh,hd->bsd', x, expert_weight)
            scale = routing_weights.sum(axis=-1, keepdims=True)
            return y * scale
        residuals = hidden_states
        logits = jnp.einsum('bsh,he->bse', hidden_states, gate_w)
        routing_weights, selected_experts = jax.lax.top_k(logits, TOPK)
        h = jnp.einsum('bsh,hi->bsi', residuals, up_w)
        h = jnp.square(jax.nn.relu(h))
        shared_out = jnp.einsum('bsi,ih->bsh', h, down_w)
        moe_out = _mock_fused_moe(hidden_states, selected_experts, routing_weights, expert_weight)
        y = shared_out + moe_out
        mu = y.mean(axis=-1, keepdims=True)
        var = jnp.mean(jnp.square(y - mu), axis=-1, keepdims=True)
        return (y - mu) * jax.lax.rsqrt(var + EPS) * ln_gamma + ln_beta
    x = x + _L0_xattn_ref(_layernorm(x, axis=-1), ctx_1024, fside_BxSx2_0, fside_BxSx2_0, L0_xattn_Wq, L0_xattn_Wkv, L0_xattn_Wout, L0_xattn_bout)
    x = x + _L0_ffn_ref(_layernorm(x, axis=-1), L0_ffn_gate_w, L0_ffn_up_w, L0_ffn_down_w, L0_ffn_expert_weight, L0_ffn_ln_gamma, L0_ffn_ln_beta)
    return x

_drawn_inputs = setup_inputs


def setup_inputs(seed=0):
    import zlib

    import numpy as np

    out = dict(_drawn_inputs(seed))
    spreads = {'L0_xattn_bout': (0.0, 0.1), 'L0_ffn_ln_gamma': (1.0, 0.2), 'L0_ffn_ln_beta': (0.0, 0.1)}
    factors = {'L0_ffn_up_w': 4.601, 'L0_ffn_down_w': 4.332}
    for name, (base, spread) in spreads.items():
        noise = np.random.default_rng([zlib.crc32(name.encode()), seed]).standard_normal(out[name].shape)
        drawn = base * np.exp(spread * noise) if base else spread * noise
        out[name] = jnp.asarray(drawn.astype(out[name].dtype))
    for name, factor in factors.items():
        out[name] = (out[name] * factor).astype(out[name].dtype)
    return out
```

```python
import numpy as np
import concourse.bass as bass
from concourse import mybir
from contextlib import ExitStack


def order(batches, groups, lag):
    steps = batches * groups
    pre = ["ln1a", "cT", "K", "ln1b", "xT", "Q"]
    stacks = ["V", "ks0", "ks1", "ks2", "ks3", "qs0", "qs1", "qs2", "qs3"]
    post = ["o0", "o1", "o2", "o3", "aT", "W", "ln2a", "-", "ln2b", "x2T", "G", "E",
            "up0", "up1", "up2", "up3", "dn", "ln3a", "-", "ln3b"]
    out = [(w, 0) for w in pre + stacks] + [("KM", 0, j) for j in range(groups // 2)]
    ahead, behind = [], []
    for b in range(1, batches):
        window = groups * (b - 1)
        ahead += [(window, w, b) for w in pre] + [(window + 4, w, b) for w in stacks]
    for b in range(batches):
        behind += [(groups * (b + 1) + lag + 1, w, b) for w in post]

    for n in range(steps + lag + 2):
        q = n - lag

        def background(k):
            for _ in range(k):
                for todo in (ahead, behind):
                    if todo and todo[0][0] <= n:
                        _, w, b = todo.pop(0)
                        if w != "-":
                            out.append((w, b))
                        break

        def scores(t):
            if n < steps:
                out.append(("S", n, t))

        def probs(i):
            if 0 <= q < steps:
                out.append(("ST", q, i))

        probs(0)
        background(1)
        if 1 <= n <= steps:
            out.append(("MT", n - 1))
        scores(0)
        probs(1)
        background(1)
        probs(2)
        scores(1)
        background(1)
        probs(3)
        background(1)
        if 0 <= q - 1 < steps:
            out.append(("PV", q - 1))
        background(1)
        b, j = divmod(q, groups)
        if j % 2 and 0 <= b < batches - 1:
            out.append(("KM", b + 1, j // 2))
    return out + [(w, b) for _, w, b in behind if w != "-"]


def xattn_ffn_kernel(nc, x, ctx_in, pos, Wq, Wkv, Wout, bout, gate_w, up_w, down_w, expert_w,
                     gamma, beta, out):
    f32, f32r = mybir.dt.float32, mybir.dt.float32r
    ALU, ACT, AX = mybir.AluOpType, mybir.ActivationFunctionType, mybir.AxisListType

    P = 128
    B, N, D = x.shape
    CD = ctx_in.shape[2]
    H, HD = 32, 8
    T = N // P
    KC = D // P
    F = up_w.shape[1]
    FT = F // P
    E = gate_w.shape[1]
    HG = 4
    G = H // HG
    Q = P // HG
    EPS = 1e-5
    SCALE = float(1.0 / np.sqrt(np.float32(HD)))
    FREQ1 = float(np.float32(10000.0) ** np.float32(-0.5))
    LAG = 3
    MROW = 3 * HD

    ORDER = order(B, G, LAG)
    BANKED = ("cT", "K", "xT", "V", "Q", "ks", "qs", "o", "aT", "W", "x2T", "G", "E", "up", "dn", "MT")
    TURN = {}
    for e in ORDER:
        if e[0].rstrip("0123") in BANKED or e[0] in BANKED:
            TURN[e] = len(TURN)

    with ExitStack() as stack:
        def sb(name, shape, dt=f32):
            return stack.enter_context(nc.sbuf_tensor(name, shape, dt))

        def bank(name):
            return stack.enter_context(nc.psum_tensor(name, [P, 512], f32))

        def sem(name):
            return stack.enter_context(nc.semaphore(name))

        x_sb = sb("x_sb", [P, B * T, D])
        c_sb = sb("c_sb", [P, B * T, CD])
        pos_sb = sb("pos_sb", [P, B * T, 2])
        wq_sb = sb("wq_sb", [P, KC, D])
        wkv_sb = sb("wkv_sb", [P, 2 * D])
        wout_sb = sb("wout_sb", [P, KC, D])
        up_sb = sb("up_sb", [P, KC, F])
        down_sb = sb("down_sb", [P, FT, D])
        exp_sb = sb("exp_sb", [P, KC, D])
        gate_sb = sb("gate_sb", [P, KC, E])
        bout_sb = sb("bout_sb", [P, D])
        gamma_sb = sb("gamma_sb", [P, D])
        beta_sb = sb("beta_sb", [P, D])
        ident = sb("ident", [P, P])
        neg_half = sb("neg_half", [P, T])
        ang = sb("ang", [P, B * T, 2, 2])
        turns = sb("turns", [P, 4 * B * T])
        wrap = sb("wrap", [P, 4 * B * T])
        arg = sb("arg", [P, 2, 4 * B * T])
        trig = sb("trig", [P, 2, 4 * B * T])
        cos8 = sb("cos8", [P, B * T, 8])
        sin8 = sb("sin8", [P, B * T, 8])
        stats = sb("stats", [P, T, 6])
        mv = sb("mv", [P, T, 2])
        var_eps = sb("var_eps", [P, T])
        rstd = sb("rstd", [P, T])
        xn = sb("xn", [P, T, D])
        xnT = sb("xnT", [P, KC, N])
        cT = sb("cT", [P, N])
        rot_c = [sb(f"rot_c{i}", [P, T, D]) for i in range(2)]
        rot_s = [sb(f"rot_s{i}", [P, T, D]) for i in range(2)]
        rot = [sb(f"rot{i}", [P, T, D]) for i in range(2)]
        nat = [sb(f"nat{i}", [P, T, H, Q]) for i in range(2)]
        kstack = sb("kstack", [P, G, N], f32r)
        kmask = sb("kmask", [P, G, HG, N], f32r)
        qstack = [sb(f"qstack{i}", [P, G, N], f32r) for i in range(2)]
        vaug = [sb(f"vaug{i}", [P, T, H, 2 * HD]) for i in range(2)]
        mneg = [sb(f"mneg{i}", [P, T, HG]) for i in range(2)]
        mnat = [sb(f"mnat{i}", [P, T, 2, HG]) for i in range(2)]
        mT = [sb(f"mT{i}", [2 * HG, N], f32r) for i in range(2)]
        probs = [sb(f"probs{i}", [P, HG, T, N]) for i in range(2)]
        oT = [sb(f"oT{i}", [P, G, N]) for i in range(2)]
        rden = sb("rden", [P, 4, H // 2])
        attn = sb("attn", [P, T, H, HD])
        attnT = sb("attnT", [P, KC, N])
        xb = sb("xb", [P, T, D])
        x2 = sb("x2", [P, T, D])
        stats2 = sb("stats2", [P, T, 6])
        mv2 = sb("mv2", [P, T, 2])
        var_eps2 = sb("var_eps2", [P, T])
        rstd2 = sb("rstd2", [P, T])
        x2n = sb("x2n", [P, T, D])
        x2b = sb("x2b", [P, T, D])
        x2nT = sb("x2nT", [P, KC, N])
        top8 = sb("top8", [P, T, 8])
        route = sb("route", [P, T])
        moe = sb("moe", [P, T, D])
        relu = [sb(f"relu{i}", [P, 2, N]) for i in range(2)]
        hT = sb("hT", [P, FT, N])
        y = sb("y", [P, T, D])
        stats3 = sb("stats3", [P, T, 6])
        mv3 = sb("mv3", [P, T, 2])
        var_eps3 = sb("var_eps3", [P, T])
        rstd3 = sb("rstd3", [P, T])
        yn = sb("yn", [P, T, D])
        fin = sb("fin", [P, T, D])

        ps_s = [bank(f"ps_s{i}") for i in range(2)]
        ps_st = [bank(f"ps_st{i}") for i in range(3)]
        ps_o = bank("ps_o")
        ps_bg = [bank(f"ps_bg{i}") for i in range(2)]

        ld_x = [sem(f"ld_x{b}") for b in range(B)]
        ld_c, ld_pos = sem("ld_c"), sem("ld_pos")
        ld_wq, ld_wkv, ld_wout, ld_ffn, ld_vec = (sem(s) for s in
                                                  ("ld_wq", "ld_wkv", "ld_wout", "ld_ffn", "ld_vec"))
        ident_ready, const_ready = sem("ident_ready"), sem("const_ready")
        arg_ready, trig_ready = sem("arg_ready"), sem("trig_ready")
        mv_ready, rstd_ready, xn_ready = sem("mv_ready"), sem("rstd_ready"), sem("xn_ready")
        mv2_ready, rstd2_ready, x2n_ready = sem("mv2_ready"), sem("rstd2_ready"), sem("x2n_ready")
        mv3_ready, rstd3_ready, yn_ready = sem("mv3_ready"), sem("rstd3_ready"), sem("yn_ready")
        bg_full = sem("bg_full")
        bg_free = [sem(f"bg_free{i}") for i in range(2)]
        nat_ready = [sem(f"nat_ready{i}") for i in range(2)]
        kmask_ready = [sem(f"kmask_ready{j}") for j in range(G // 2)]
        s_full, s_free, mnat_ready = sem("s_full"), sem("s_free"), sem("mnat_ready")
        m_sent = [sem(f"m_sent{i}") for i in range(2)]
        st_full, st_free, pv_done, oT_ready = sem("st_full"), sem("st_free"), sem("pv_done"), sem("oT_ready")
        xb_ready, x2b_ready, h_ready, fin_ready = sem("xb_ready"), sem("x2b_ready"), sem("h_ready"), sem("fin_ready")
        out_done = sem("out_done")
        ps_o_zeroed = sem("ps_o_zeroed")
        dve_chain, pool_chain = sem("dve_chain"), sem("pool_chain")

        def bg(e):
            return ps_bg[TURN[e] % 2]

        def full(e):
            return TURN[e] + 1

        def emptied(ins, e):
            return ins.then_inc(bg_free[TURN[e] % 2], 1)

        def taken(eng, e):
            eng.wait_ge(bg_free[TURN[e] % 2], TURN[e] // 2 + 1)

        def step(n):
            return n // G, n % G

        block = stack.enter_context(nc.Block())

        @block.sync
        def _(sp):
            xv = x.rearrange("b (t p) d -> p (b t) d", p=P)
            sp.dma_start(c_sb[:], ctx_in.rearrange("b (t p) d -> p (b t) d", p=P)).then_inc(ld_c, 16)
            sp.dma_start(x_sb[:, 0:T, :], xv[:, 0:T, :]).then_inc(ld_x[0], 16)
            sp.dma_start(wkv_sb[:], Wkv).then_inc(ld_wkv, 16)
            sp.dma_start(wq_sb[:], Wq.rearrange("(k p) n -> p k n", p=P)).then_inc(ld_wq, 16)
            for b in range(1, B):
                sp.dma_start(x_sb[:, b * T:(b + 1) * T, :], xv[:, b * T:(b + 1) * T, :]).then_inc(ld_x[b], 16)
            for e in ORDER:
                if e[0] == "KM":
                    b, j = e[1], e[2]
                    groups = slice(2 * j, 2 * j + 2)
                    taken(sp, (f"ks{j}", b))
                    if b == 0:
                        sp.wait_ge(const_ready, 3)
                    else:
                        sp.wait_ge(st_full, HG * (G * (b - 1) + 2 * j + 2))
                    for i in range(HG):
                        sp.dma_start(kmask[Q * i:Q * (i + 1), groups, i, :].bitcast(f32),
                                     kstack[Q * i:Q * (i + 1), groups, :].bitcast(f32)).then_inc(kmask_ready[j], 16)
                elif e[0] == "MT":
                    n = e[1]
                    b, g = step(n)
                    taken(sp, e)
                    sp.wait_ge(s_full, 4 * (n + 1))
                    for part in range(2):
                        sp.dma_start(qstack[b % 2][MROW + part::Q, g, :].bitcast(f32),
                                     mT[n % 2][HG * part:HG * (part + 1), :].bitcast(f32)).then_inc(m_sent[n % 2], 16)
                elif e[0] == "ln3b":
                    b = e[1]
                    sp.wait_ge(fin_ready, b + 1)
                    sp.dma_start(out[b].rearrange("(t p) d -> p t d", p=P), fin[:]).then_inc(out_done, 16)
            sp.wait_ge(out_done, 16 * B)

        @block.gpsimd
        def _(pool):
            chain = [0]

            def link(ins):
                chain[0] += 1
                ins.then_inc(pool_chain, 1)
                pool.wait_ge(pool_chain, chain[0])

            pool.dma_start(wout_sb[:], Wout.rearrange("(k p) n -> p k n", p=P)).then_inc(ld_wout, 16)
            pool.dma_start(up_sb[:], up_w.rearrange("(k p) n -> p k n", p=P)).then_inc(ld_ffn, 16)
            pool.dma_start(down_sb[:], down_w.rearrange("(k p) n -> p k n", p=P)).then_inc(ld_ffn, 16)
            pool.dma_start(exp_sb[:], expert_w.rearrange("(k p) n -> p k n", p=P)).then_inc(ld_ffn, 16)
            pool.dma_start(gate_sb[:], gate_w.rearrange("(k p) n -> p k n", p=P)).then_inc(ld_ffn, 16)
            link(pool.memset(ident[:], 0.0))
            pool.affine_select(out=ident[:], in_=ident[:], compare_op=ALU.not_equal, fill=1.0, base=0,
                               pattern=[[-1, P]], channel_multiplier=1).then_inc(ident_ready, 1)
            link(pool.memset(neg_half[:], -0.5))
            for i in range(2):
                link(pool.memset(nat[i][:, :, :, MROW:Q], 0.0))
            pool.memset(nat[0][:, :, :, MROW:MROW + 2], 1.0).then_inc(pool_chain, 1)
            chain[0] += 1
            for i in range(2):
                pool.memset(vaug[i][:, :, :, HD:2 * HD], 1.0).then_inc(const_ready, 1)
            pool.memset(kmask[:].bitcast(f32), 0.0).then_inc(const_ready, 1)

            def inverse_deviation(mean_var, plus_eps, result, ready, done, b):
                pool.wait_ge(ready, b + 1)
                link(pool.tensor_scalar(plus_eps[:], mean_var[:, :, 1], EPS, None, ALU.add))
                pool.tensor_tensor(result[:], plus_eps[:], neg_half[:], ALU.pow).then_inc(done, 1)

            def stack_rows(which, b):
                taken(pool, (("K", "Q")[which], b))
                swapped = rot_s[which][:].rearrange("p t (a two) -> p (t a) two", two=2)[:, :, ::-1]
                link(pool.tensor_tensor(rot[which][:].rearrange("p t (a two) -> p (t a) two", two=2),
                                        rot_c[which][:].rearrange("p t (a two) -> p (t a) two", two=2),
                                        swapped, ALU.add))
                if b >= 1:
                    last = ("qs3" if which else "ks3", b - 1)
                    pool.wait_ge(bg_full, full(last))
                r = rot[which][:].rearrange("p t (h d) -> p (t h) d", d=HD)
                rows = nat[which][:].rearrange("p t h r -> p (t h) r")
                hi, lo, again = (0, 1, 2) if which else (0, 2, 1)
                at = lambda k: rows[:, :, k * HD:(k + 1) * HD]
                pool.tensor_scalar(at(again).bitcast(f32r), r, 1.0, 0.0, ALU.mult, ALU.add).then_inc(pool_chain, 1)
                chain[0] += 1
                link(pool.tensor_scalar(at(hi).bitcast(f32r), r, 1.0, 0.0, ALU.mult, ALU.add))
                pool.tensor_tensor(at(lo).bitcast(f32r), r, at(hi), ALU.subtract).then_inc(nat_ready[which], 1)

            for e in ORDER:
                what, b = e[0], e[1]
                if what == "ln1a":
                    inverse_deviation(mv, var_eps, rstd, mv_ready, rstd_ready, b)
                elif what == "K":
                    stack_rows(0, b)
                elif what == "Q":
                    stack_rows(1, b)
                elif what == "o0":
                    if b == 0:
                        pool.wait_ge(ld_vec, 48)
                    if b >= 1:
                        taken(pool, ("W", b - 1))
                    pool.tensor_tensor(xb[:], x_sb[:, b * T:(b + 1) * T, :],
                                       bout_sb[:].unsqueeze(1).broadcast_to((P, T, D)), ALU.add).then_inc(xb_ready, 1)
                elif what == "ln2a":
                    inverse_deviation(mv2, var_eps2, rstd2, mv2_ready, rstd2_ready, b)
                    taken(pool, ("W", b))
                    if b >= 1:
                        pool.wait_ge(fin_ready, b)
                    pool.tensor_tensor(x2b[:], x2[:], beta_sb[:].unsqueeze(1).broadcast_to((P, T, D)),
                                       ALU.add).then_inc(x2b_ready, 1)
                elif what[:2] == "up":
                    j = int(what[2])
                    taken(pool, e)
                    if b >= 1 and j == 0:
                        pool.wait_ge(bg_full, full(("dn", b - 1)))
                    pool.tensor_tensor(hT[:, 2 * j:2 * j + 2, :], relu[j % 2][:], relu[j % 2][:],
                                       ALU.mult).then_inc(h_ready, 1)
                elif what == "ln3a":
                    inverse_deviation(mv3, var_eps3, rstd3, mv3_ready, rstd3_ready, b)
                elif what == "ln3b":
                    pool.wait_ge(yn_ready, b + 1)
                    link(pool.tensor_tensor(yn[:], yn[:], gamma_sb[:].unsqueeze(1).broadcast_to((P, T, D)), ALU.mult))
                    if b >= 1:
                        pool.wait_ge(out_done, 16 * b)
                    pool.tensor_tensor(fin[:], yn[:], x2b[:], ALU.add).then_inc(fin_ready, 1)

        @block.scalar
        def _(act):
            act.dma_start(pos_sb[:], pos.rearrange("b (t p) a -> p (b t) a", p=P)).then_inc(ld_pos, 16)
            for v, t in ((bout, bout_sb), (gamma, gamma_sb), (beta, beta_sb)):
                act.dma_start(t[:], v.rearrange("(a d) -> a d", a=1).broadcast_to((P, D))).then_inc(ld_vec, 16)
            act.wait_ge(arg_ready, 1)
            act.activation(trig[:], arg[:], ACT.Sin).then_inc(trig_ready, 1)

            def copy(e, to, of):
                act.wait_ge(bg_full, full(e))
                emptied(act.activation(to, of, ACT.Copy), e)

            for e in ORDER:
                what, b = e[0], e[1]
                if what == "cT":
                    if b >= 1:
                        act.wait_ge(bg_full, full(("V", b - 1)))
                    copy(e, cT[:], bg(e)[:, 0:N])
                elif what == "xT":
                    if b >= 1:
                        act.wait_ge(bg_full, full(("Q", b - 1)))
                    copy(e, xnT[:], bg(e)[:].rearrange("p (k n) -> p k n", k=KC))
                elif what == "V":
                    if b == 0:
                        act.wait_ge(const_ready, 2)
                    if b >= 2:
                        act.wait_ge(pv_done, G * (b - 1))
                    copy(e, vaug[b % 2][:, :, :, 0:HD], bg(e)[:].rearrange("p (t h d) -> p t h d", t=T, h=H))
                elif what[:2] == "ks":
                    j = int(what[2])
                    if b >= 1:
                        act.wait_ge(kmask_ready[j], 64 * b)
                    copy(e, kstack[:, 2 * j:2 * j + 2, :], bg(e)[:].rearrange("p (g n) -> p g n", g=2))
                elif what[:2] == "qs":
                    j = int(what[2])
                    if b >= 2 and j == 0:
                        act.wait_ge(st_full, HG * G * (b - 1))
                    copy(e, qstack[b % 2][:, 2 * j:2 * j + 2, :], bg(e)[:].rearrange("p (g n) -> p g n", g=2))
                elif what == "ST":
                    n, i = e[1], e[2]
                    k = HG * n + i
                    act.wait_ge(st_full, k + 1)
                    if i == 0 and n >= 2:
                        act.wait_ge(pv_done, n - 1)
                    act.activation(probs[n % 2][:, i, :, :], ps_st[k % 3][:].rearrange("p (t n) -> p t n", t=T),
                                   ACT.Exp, scale=SCALE).then_inc(st_free, 1)
                elif what == "PV":
                    n = e[1]
                    b, g = step(n)
                    act.wait_ge(pv_done, n + 1)
                    if g == 0 and b >= 2:
                        act.wait_ge(bg_full, full(("o3", b - 2)))
                    act.activation(oT[b % 2][:, g, :], ps_o[:, 0:N], ACT.Copy).then_inc(oT_ready, 1)
                elif what == "aT":
                    if b >= 1:
                        act.wait_ge(bg_full, full(("W", b - 1)))
                    copy(e, attnT[:], bg(e)[:].rearrange("p (k n) -> p k n", k=KC))
                elif what == "x2T":
                    if b >= 1:
                        act.wait_ge(bg_full, full(("dn", b - 1)))
                    copy(e, x2nT[:], bg(e)[:].rearrange("p (k n) -> p k n", k=KC))
                elif what == "E":
                    taken(act, ("G", b))
                    act.wait_ge(bg_full, full(e))
                    if b >= 1:
                        act.wait_ge(mv3_ready, b)
                    for t in range(T):
                        ins = act.activation(moe[:, t, :], bg(e)[:, t * D:(t + 1) * D], ACT.Copy,
                                             scale=route[:, t:t + 1])
                    emptied(ins, e)
                elif what[:2] == "up":
                    j = int(what[2])
                    k = 4 * b + j
                    act.wait_ge(bg_full, full(e))
                    if k >= 2:
                        act.wait_ge(h_ready, k - 1)
                    emptied(act.activation(relu[j % 2][:], bg(e)[:].rearrange("p (f n) -> p f n", f=2), ACT.Relu), e)

        @block.vector
        def _(dve):
            chain = [0]

            def link(ins):
                chain[0] += 1
                ins.then_inc(dve_chain, 1)
                dve.wait_ge(dve_chain, chain[0])

            def mean_variance(source, st, result, ready):
                for t in range(T):
                    ins = dve.bn_stats(st[:, t, :], source[:, t, :])
                link(ins)
                for t in range(T):
                    ins = dve.bn_aggr(result[:, t, :], st[:, t, :])
                ins.then_inc(ready, 1)

            def normalise(to, source, mean_var, r, done):
                for t in range(T):
                    ins = dve.tensor_scalar(to[:, t, :], source[:, t, :], mean_var[:, t, 0:1], r[:, t:t + 1],
                                            ALU.subtract, ALU.mult)
                ins.then_inc(done, 1)

            def rotary_tables():
                dve.wait_ge(ld_pos, 16)
                dve.tensor_copy(ang[:, :, :, 0], pos_sb[:])
                link(dve.tensor_scalar(ang[:, :, :, 1], pos_sb[:], FREQ1, None, ALU.mult))
                a = ang[:].rearrange("p n x f -> p (n x f)")
                magic = 1.5 * 2.0 ** 23
                two_pi = 2 * np.pi
                c1 = float(np.float32(6.28125))
                c2 = float(np.float32(two_pi - c1))
                c3 = float(np.float32(two_pi - c1 - c2))
                pi = float(np.nextafter(np.float32(np.pi), np.float32(0)))
                link(dve.tensor_scalar(turns[:], a, float(1 / two_pi), magic, ALU.mult, ALU.add))
                link(dve.tensor_scalar(turns[:], turns[:], magic, None, ALU.subtract))
                link(dve.scalar_tensor_tensor(out=a, in0=turns[:], scalar=-c1, in1=a, op0=ALU.mult, op1=ALU.add))
                link(dve.scalar_tensor_tensor(out=a, in0=turns[:], scalar=-c2, in1=a, op0=ALU.mult, op1=ALU.add))
                link(dve.scalar_tensor_tensor(out=a, in0=turns[:], scalar=-c3, in1=a, op0=ALU.mult, op1=ALU.add))
                dve.tensor_scalar(arg[:, 0, :], a, pi, -pi, ALU.min, ALU.max)
                link(dve.tensor_scalar(turns[:], a, float(np.pi / 2), None, ALU.add))
                link(dve.tensor_scalar(wrap[:], turns[:], pi, -two_pi, ALU.is_gt, ALU.mult))
                link(dve.tensor_tensor(turns[:], turns[:], wrap[:], ALU.add))
                dve.tensor_scalar(arg[:, 1, :], turns[:], pi, -pi, ALU.min, ALU.max).then_inc(arg_ready, 1)
                dve.wait_ge(trig_ready, 1)
                pairs = lambda t: t[:].rearrange("p n (f two) -> p (n f) two", two=2)
                dve.tensor_copy(pairs(cos8), trig[:, 1, :].unsqueeze(2).broadcast_to((P, 4 * B * T, 2)))
                dve.tensor_copy(pairs(sin8)[:, :, 0], trig[:, 0, :])
                link(dve.tensor_scalar(pairs(sin8)[:, :, 1], trig[:, 0, :], -1.0, None, ALU.mult))

            def rotate(e, which, b):
                dve.wait_ge(bg_full, full(e))
                if b >= 1:
                    dve.wait_ge(nat_ready[which], b)
                source = bg(e)[:].rearrange("p (t h d) -> p t h d", t=T, h=H)
                table = lambda w: w[:, b * T:(b + 1) * T, :].unsqueeze(2).broadcast_to((P, T, H, 8))
                by_head = lambda w: w[:].rearrange("p t (h d) -> p t h d", h=H)
                dve.tensor_tensor(by_head(rot_c[which]), source, table(cos8), ALU.mult)
                emptied(dve.tensor_tensor(by_head(rot_s[which]), source, table(sin8), ALU.mult), e)

            dve.memset(ps_o[:], 0.0).then_inc(ps_o_zeroed, 1)
            for e in ORDER:
                what, b = e[0], e[1]
                if what == "ln1a":
                    dve.wait_ge(ld_x[b], 16)
                    if b >= 1:
                        dve.wait_ge(rstd_ready, b)
                    mean_variance(x_sb[:, b * T:(b + 1) * T, :], stats, mv, mv_ready)
                    if b == 0:
                        rotary_tables()
                elif what == "K":
                    rotate(e, 0, b)
                elif what == "ln1b":
                    dve.wait_ge(rstd_ready, b + 1)
                    if b >= 1:
                        dve.wait_ge(bg_full, full(("xT", b - 1)))
                    normalise(xn, x_sb[:, b * T:(b + 1) * T, :], mv, rstd, xn_ready)
                elif what == "Q":
                    rotate(e, 1, b)
                elif what == "S":
                    n, t = e[1], e[2]
                    if t == 0 and n >= 2:
                        dve.wait_ge(bg_full, full(("MT", n - 2)))
                    for half in range(2):
                        dve.wait_ge(s_full, 4 * n + 2 * t + half + 1)
                        ins = dve.tensor_reduce(mneg[n % 2][:, t, 2 * half:2 * half + 2],
                                                ps_s[half][:].rearrange("p (i k) -> p i k", i=2),
                                                AX.X, ALU.max, negate=True).then_inc(s_free, 1)
                    if t == T - 1:
                        dve.wait_ge(s_free, 4 * (n + 1))
                        link(dve.tensor_copy(mnat[n % 2][:, :, 0, :].bitcast(f32r), mneg[n % 2][:]))
                        dve.tensor_tensor(mnat[n % 2][:, :, 1, :].bitcast(f32r), mneg[n % 2][:], mnat[n % 2][:, :, 0, :],
                                          ALU.subtract).then_inc(mnat_ready, 1)
                elif what == "MT":
                    n = e[1]
                    dve.wait_ge(bg_full, full(e))
                    if n >= 2:
                        dve.wait_ge(m_sent[n % 2], 32 * (n // 2))
                    emptied(dve.tensor_copy(mT[n % 2][:], bg(e)[0:2 * HG, 0:N]), e)
                elif what[0] == "o":
                    t, half = int(what[1]) // 2, int(what[1]) % 2
                    dve.wait_ge(bg_full, full(e))
                    if b >= 1 and what == "o0":
                        dve.wait_ge(bg_full, full(("aT", b - 1)))
                    o = bg(e)[:].rearrange("p (h r) -> p h r", r=Q)
                    r = rden[:, 2 * t + half, :]
                    if b >= 1:
                        taken(dve, (what, b - 1))
                    link(dve.reciprocal(r, o[:, :, HD]))
                    emptied(dve.tensor_tensor(attn[:, t, half * H // 2:(half + 1) * H // 2, :], o[:, :, 0:HD],
                                              r.unsqueeze(2).broadcast_to((P, H // 2, HD)), ALU.mult), e)
                elif what == "W":
                    dve.wait_ge(bg_full, full(e))
                    dve.wait_ge(xb_ready, b + 1)
                    if b >= 1:
                        dve.wait_ge(x2n_ready, b)
                        dve.wait_ge(x2b_ready, b)
                    emptied(dve.tensor_tensor(x2[:], bg(e)[:].rearrange("p (t d) -> p t d", t=T), xb[:], ALU.add), e)
                elif what == "ln2a":
                    taken(dve, ("W", b))
                    if b >= 1:
                        dve.wait_ge(rstd2_ready, b)
                    mean_variance(x2, stats2, mv2, mv2_ready)
                elif what == "ln2b":
                    dve.wait_ge(rstd2_ready, b + 1)
                    if b >= 1:
                        dve.wait_ge(bg_full, full(("x2T", b - 1)))
                    normalise(x2n, x2, mv2, rstd2, x2n_ready)
                elif what == "G":
                    dve.wait_ge(bg_full, full(e))
                    for t in range(T):
                        ins = dve.max(top8[:, t, :], bg(e)[:, t * E:(t + 1) * E])
                    link(ins)
                    if b >= 1:
                        taken(dve, ("E", b - 1))
                    emptied(dve.tensor_tensor(route[:], top8[:, :, 0], top8[:, :, 1], ALU.add), e)
                elif what == "dn":
                    dve.wait_ge(bg_full, full(e))
                    taken(dve, ("E", b))
                    emptied(dve.tensor_tensor(y[:], bg(e)[:].rearrange("p (t d) -> p t d", t=T), moe[:], ALU.add), e)
                elif what == "ln3a":
                    taken(dve, ("dn", b))
                    if b >= 1:
                        dve.wait_ge(rstd3_ready, b)
                    mean_variance(y, stats3, mv3, mv3_ready)
                elif what == "ln3b":
                    dve.wait_ge(rstd3_ready, b + 1)
                    if b >= 1:
                        dve.wait_ge(fin_ready, b)
                    normalise(yn, y, mv3, rstd3, yn_ready)

        @block.tensor
        def _(pe):
            def begin(e):
                k = TURN[e]
                if k >= 2:
                    pe.wait_ge(bg_free[k % 2], k // 2)

            def transposes(e, blocks):
                begin(e)
                at = 0
                for block_ in blocks:
                    m = block_.shape[0]
                    ins = pe.transpose(bg(e)[0:block_.shape[1], at:at + m], block_, ident[:])
                    at += m
                ins.then_inc(bg_full, 1)

            def by_token(e, lhs, rhs, cols):
                begin(e)
                for t in range(T):
                    for k in range(len(rhs)):
                        ins = pe.matmul(bg(e)[:, t * cols:(t + 1) * cols], lhs[k][:, t * P:(t + 1) * P], rhs[k],
                                        start=(k == 0), stop=(k == len(rhs) - 1))
                ins.then_inc(bg_full, 1)

            def tiles(buffer, count):
                return [buffer[:, k, :] for k in range(count)]

            pe.wait_ge(ident_ready, 1)
            for e in ORDER:
                what, b = e[0], e[1]
                if what == "cT":
                    if b == 0:
                        pe.wait_ge(ld_c, 16)
                    transposes(e, [c_sb[:, b * T + t, :] for t in range(T)])
                elif what == "K":
                    if b == 0:
                        pe.wait_ge(ld_wkv, 16)
                    taken(pe, ("cT", b))
                    by_token(e, [cT], [wkv_sb[:, 0:D]], D)
                elif what == "V":
                    by_token(e, [cT], [wkv_sb[:, D:2 * D]], D)
                elif what == "xT":
                    pe.wait_ge(xn_ready, b + 1)
                    transposes(e, [xn[:, t, k * P:(k + 1) * P] for k in range(KC) for t in range(T)])
                elif what == "Q":
                    if b == 0:
                        pe.wait_ge(ld_wq, 16)
                    taken(pe, ("xT", b))
                    by_token(e, tiles(xnT, KC), tiles(wq_sb, KC), D)
                elif what[:2] in ("ks", "qs"):
                    which, j = int(what[0] == "q"), int(what[2])
                    if j == 0:
                        pe.wait_ge(nat_ready[which], b + 1)
                    rows = nat[which][:].rearrange("p t (g i) r -> p t g (i r)", g=G)
                    transposes(e, [rows[:, t, g, :] for g in (2 * j, 2 * j + 1) for t in range(T)])
                elif what == "S":
                    n, t = e[1], e[2]
                    b, g = step(n)
                    if g % 2 == 0 and t == 0:
                        pe.wait_ge(kmask_ready[g // 2], 64 * (b + 1))
                        taken(pe, (f"qs{g // 2}", b))
                    for half in range(2):
                        k = 4 * n + 2 * t + half
                        if k >= 2:
                            pe.wait_ge(s_free, k - 1)
                        pe.matmul(ps_s[half][:], qstack[b % 2][:, g, t * P:(t + 1) * P],
                                  kmask[:, g, 2 * half:2 * half + 2, :], start=True, stop=True)\
                            .then_inc(s_full, 1)
                elif what == "MT":
                    n = e[1]
                    pe.wait_ge(mnat_ready, n + 1)
                    transposes(e, [mnat[n % 2][:, t, :, :].rearrange("p a i -> p (a i)") for t in range(T)])
                elif what == "ST":
                    n, i = e[1], e[2]
                    b, g = step(n)
                    k = HG * n + i
                    if i == 0:
                        pe.wait_ge(m_sent[n % 2], 32 * (n // 2 + 1))
                    if k >= 3:
                        pe.wait_ge(st_free, k - 2)
                    for t in range(T):
                        ins = pe.matmul(ps_st[k % 3][:, t * N:(t + 1) * N], kmask[:, g, i, t * P:(t + 1) * P],
                                        qstack[b % 2][:, g, :], start=True, stop=True)
                    ins.then_inc(st_full, 1)
                elif what == "PV":
                    n = e[1]
                    b, g = step(n)
                    pe.wait_ge(st_free, HG * (n + 1))
                    if n == 0:
                        pe.wait_ge(ps_o_zeroed, 1)
                    else:
                        pe.wait_ge(oT_ready, n)
                    if g == 0:
                        taken(pe, ("V", b))
                    for t in range(T):
                        for i in range(HG):
                            ins = pe.matmul(ps_o[Q * i:Q * i + 2 * HD, 0:N], vaug[b % 2][:, t, HG * g + i, :],
                                            probs[n % 2][:, i, t, :], start=(t == 0), stop=(t == T - 1))
                    ins.then_inc(pv_done, 1)
                elif what[0] == "o":
                    t, half = int(what[1]) // 2, int(what[1]) % 2
                    pe.wait_ge(oT_ready, G * (b + 1))
                    transposes(e, [oT[b % 2][:, half * G // 2 + j, t * P:(t + 1) * P] for j in range(G // 2)])
                elif what == "aT":
                    taken(pe, ("o3", b))
                    rows = attn[:].rearrange("p t h d -> p t (h d)")
                    transposes(e, [rows[:, t, k * P:(k + 1) * P] for k in range(KC) for t in range(T)])
                elif what == "W":
                    if b == 0:
                        pe.wait_ge(ld_wout, 16)
                    taken(pe, ("aT", b))
                    by_token(e, tiles(attnT, KC), tiles(wout_sb, KC), D)
                elif what == "x2T":
                    pe.wait_ge(x2n_ready, b + 1)
                    transposes(e, [x2n[:, t, k * P:(k + 1) * P] for k in range(KC) for t in range(T)])
                elif what == "G":
                    if b == 0:
                        pe.wait_ge(ld_ffn, 64)
                    taken(pe, ("x2T", b))
                    by_token(e, tiles(x2nT, KC), tiles(gate_sb, KC), E)
                elif what == "E":
                    by_token(e, tiles(x2nT, KC), tiles(exp_sb, KC), D)
                elif what[:2] == "up":
                    j = int(what[2])
                    begin(e)
                    for f in range(2):
                        for k in range(KC):
                            ins = pe.matmul(bg(e)[:, f * N:(f + 1) * N],
                                            up_sb[:, k, (2 * j + f) * P:(2 * j + f + 1) * P], x2nT[:, k, :],
                                            start=(k == 0), stop=(k == KC - 1))
                    ins.then_inc(bg_full, 1)
                elif what == "dn":
                    pe.wait_ge(h_ready, 4 * (b + 1))
                    by_token(e, tiles(hT, FT), tiles(down_sb, FT), D)


_INS = ["x", "ctx_1024", "fside_BxSx2_0", "L0_xattn_Wq", "L0_xattn_Wkv", "L0_xattn_Wout", "L0_xattn_bout",
        "L0_ffn_gate_w", "L0_ffn_up_w", "L0_ffn_down_w", "L0_ffn_expert_weight", "L0_ffn_ln_gamma",
        "L0_ffn_ln_beta"]


def kernel(**inputs):
    import numpy as _np
    import concourse.bacc as _bacc
    from concourse import mybir as _mybir
    from concourse.bass_utils import run_bass_kernel_spmd as _run

    nc = _bacc.Bacc("TRN2", target_bir_lowering=False, num_devices=1)
    arrays, args = {}, []
    for name in _INS:
        a = _np.ascontiguousarray(inputs[name])
        arrays[f"in_{name}"] = a
        args.append(nc.dram_tensor(f"in_{name}", a.shape, _mybir.dt.from_np(a.dtype), kind="ExternalInput").ap())
    result = nc.dram_tensor("result", inputs["x"].shape, _mybir.dt.float32, kind="ExternalOutput").ap()
    xattn_ffn_kernel(nc, *args, result)
    r = _run(nc, [arrays], core_ids=[0])
    return r.results[0]["result"]
```

```python
import numpy as np
import concourse.bass as bass
from concourse import mybir
from contextlib import ExitStack


def order(batches, groups, lag):
    steps = batches * groups
    pre = ["ln1a", "cT", "-", "ln1b", "K", "-", "xT", "-", "Q"]
    stacks = ["V", "ks0", "ks1", "ks2", "ks3", "qs0", "qs1", "qs2", "qs3"]
    post = ["o0", "o1", "o2", "o3", "-", "aT", "-", "W", "-", "ln2a", "-", "-", "ln2b", "-", "x2T", "-",
            "up0", "up1", "up2", "up3", "E0", "E1", "dn", "-", "ln3a", "-", "-", "ln3b"]
    out = [(w, 0) for w in pre + stacks if w != "-"] + [("KM", 0, j) for j in range(groups // 2)]
    ahead, behind = [], []
    for b in range(1, batches):
        window = groups * (b - 1)
        ahead += [(window + 2, w, b) for w in pre] + [(window + lag + 1, w, b) for w in stacks]
    for b in range(batches):
        behind += [(groups * (b + 1) + lag + 1, w, b) for w in post]

    for n in range(steps + lag + 2):
        q = n - lag

        def background():
            for todo in (ahead, behind):
                if todo and todo[0][0] <= n:
                    _, w, b = todo.pop(0)
                    if w != "-":
                        out.append((w, b))

        for k in range(4):
            if 0 <= q < steps:
                out.append(("ST", q, k))
            if n < steps:
                out.append(("S", n, k))
            background()
            if k == 0 and n % 2 == 0 and 2 <= n <= steps:
                out.append(("MT", n // 2 - 1))
        if 0 <= q - 1 < steps:
            out.append(("PV", q - 1))
        background()
        b, j = divmod(q, groups)
        if j % 2 and 0 <= b < batches - 1:
            out.append(("KM", b + 1, j // 2))
    return out + [(w, b) for _, w, b in behind if w != "-"]


def xattn_ffn_kernel(nc, x, ctx_in, pos, Wq, Wkv, Wout, bout, gate_w, up_w, down_w, expert_w,
                     gamma, beta, out):
    f32, f32r = mybir.dt.float32, mybir.dt.float32r
    ALU, ACT, AX = mybir.AluOpType, mybir.ActivationFunctionType, mybir.AxisListType

    P = 128
    B, N, D = x.shape
    CD = ctx_in.shape[2]
    H, HD = 32, 8
    T = N // P
    KC = D // P
    F = up_w.shape[1]
    FT = F // P
    E = gate_w.shape[1]
    HG = 4
    G = H // HG
    Q = P // HG
    EPS = 1e-5
    SCALE = float(1.0 / np.sqrt(np.float32(HD)))
    FREQ1 = float(np.float32(10000.0) ** np.float32(-0.5))
    LAG = 4
    WS = 2 + KC * F // 512
    MROW = 3 * HD

    ORDER = order(B, G, LAG)
    BANKED = ("cT", "K", "xT", "V", "Q", "ks", "qs", "o", "aT", "W", "x2T", "E", "up", "dn", "MT")
    TURN = {}
    for e in ORDER:
        if e[0].rstrip("0123") in BANKED or e[0] in BANKED:
            TURN[e] = len(TURN)
    SPLIT = {e: k for k, e in enumerate(e for e in ORDER if e[0] in ("cT", "xT", "aT", "x2T"))}

    with ExitStack() as stack:
        def sb(name, shape, dt=f32):
            return stack.enter_context(nc.sbuf_tensor(name, shape, dt))

        def bank(name):
            return stack.enter_context(nc.psum_tensor(name, [P, 512], f32))

        def sem(name):
            return stack.enter_context(nc.semaphore(name))

        x_sb = sb("x_sb", [P, B * T, D])
        c_sb = sb("c_sb", [P, B * T, CD])
        pos_sb = sb("pos_sb", [P, B * T, 2])
        wq = sb("wq", [P, 2, KC, D], f32r)
        wkv = sb("wkv", [P, 2, 1, 2 * D], f32r)
        wout = sb("wout", [P, 2, KC, D], f32r)
        up = sb("up", [P, 2, KC, F], f32r)
        expert = sb("expert", [P, 2, KC, D + E], f32r)
        down_sb = sb("down_sb", [P, FT, D])
        bout_sb = sb("bout_sb", [P, D])
        gamma_sb = sb("gamma_sb", [P, D])
        beta_sb = sb("beta_sb", [P, D])
        ident = sb("ident", [P, P])
        neg_half = sb("neg_half", [P, T])
        ang = sb("ang", [P, B * T, 2, 2])
        turns = sb("turns", [P, 4 * B * T])
        wrap = sb("wrap", [P, 4 * B * T])
        arg = sb("arg", [P, 2, 4 * B * T])
        trig = sb("trig", [P, 2, 4 * B * T])
        cos8 = sb("cos8", [P, B * T, 8])
        sin8 = sb("sin8", [P, B * T, 8])
        stats = sb("stats", [P, T, 6])
        mv = sb("mv", [P, T, 2])
        var_eps = sb("var_eps", [P, T])
        rstd = sb("rstd", [P, T])
        xn = sb("xn", [P, T, D])
        xnT = sb("xnT", [P, 2, KC, N], f32r)
        cT = sb("cT", [P, 2, 1, N], f32r)
        rot_c = [sb(f"rot_c{i}", [P, T, D]) for i in range(2)]
        rot_s = [sb(f"rot_s{i}", [P, T, D]) for i in range(2)]
        nat = [sb(f"nat{i}", [P, T, H, Q]) for i in range(2)]
        kstack = sb("kstack", [P, G, N], f32r)
        kmask = sb("kmask", [P, G, HG, N], f32r)
        qstack = [sb(f"qstack{i}", [P, G, N], f32r) for i in range(2)]
        vaug = [sb(f"vaug{i}", [P, T, H, 2 * HD]) for i in range(2)]
        mneg = [sb(f"mneg{i}", [P, T, 2, HG]) for i in range(2)]
        mnat = [sb(f"mnat{i}", [P, T, 2, HG * 2]) for i in range(2)]
        mT = [sb(f"mT{i}", [2 * HG * 2, N], f32r) for i in range(2)]
        probs = [sb(f"probs{i}", [P, HG, T, N]) for i in range(2)]
        oT = sb("oT", [P, G, N])
        rden = sb("rden", [P, 4, H // 2])
        attn = sb("attn", [P, T, H, HD])
        attnT = sb("attnT", [P, 2, KC, N], f32r)
        stats2 = sb("stats2", [P, T, 6])
        mv2 = sb("mv2", [P, T, 2])
        var_eps2 = sb("var_eps2", [P, T])
        rstd2 = sb("rstd2", [P, T])
        x2n = sb("x2n", [P, T, D])
        x2nT = sb("x2nT", [P, 2, KC, N], f32r)
        top8 = sb("top8", [P, T, 8])
        route = sb("route", [P, T])
        moe = sb("moe", [P, T, D])
        y_fin = sb("y_fin", [P, 2 * T * D])
        y, fin = (y_fin[:, i * T * D:(i + 1) * T * D].rearrange("p (t d) -> p t d", t=T) for i in range(2))
        hT = sb("hT", [P, FT, N])
        raw_q, raw_kv = rot_c[1], rot_s[1]
        raw_up = hT[:].rearrange("p f n -> p (f n)").rearrange("p (k n) -> p k n", k=KC)
        raw_out = moe
        raw_expert = y_fin[:, 0:KC * (D + E)].rearrange("p (k n) -> p k n", k=KC)
        stats3 = sb("stats3", [P, T, 6])
        mv3 = sb("mv3", [P, T, 2])
        var_eps3 = sb("var_eps3", [P, T])
        rstd3 = sb("rstd3", [P, T])

        ps_s = [bank(f"ps_s{i}") for i in range(2)]
        ps_st = [bank(f"ps_st{i}") for i in range(3)]
        ps_o = bank("ps_o")
        ps_bg = [bank(f"ps_bg{i}") for i in range(2)]

        ld_x = [sem(f"ld_x{b}") for b in range(B)]
        ld_c = [sem(f"ld_c{b}") for b in range(B)]
        ld_pos, ld_down = sem("ld_pos"), sem("ld_down")
        ld_wq, ld_wkv, ld_wout, ld_ffn, ld_vec = (sem(s) for s in
                                                  ("ld_wq", "ld_wkv", "ld_wout", "ld_ffn", "ld_vec"))
        ident_ready, const_ready = sem("ident_ready"), sem("const_ready")
        arg_ready, trig_ready = sem("arg_ready"), sem("trig_ready")
        mv_ready, rstd_ready, xn_ready = sem("mv_ready"), sem("rstd_ready"), sem("xn_ready")
        mv2_ready, rstd2_ready, x2n_ready = sem("mv2_ready"), sem("rstd2_ready"), sem("x2n_ready")
        mv3_ready, rstd3_ready, yn_ready = sem("mv3_ready"), sem("rstd3_ready"), sem("yn_ready")
        bg_full = sem("bg_full")
        bg_free = [sem(f"bg_free{i}") for i in range(2)]
        nat_ready = [sem(f"nat_ready{i}") for i in range(2)]
        kmask_ready = [sem(f"kmask_ready{j}") for j in range(G // 2)]
        s_full, s_free, mnat_ready = sem("s_full"), sem("s_free"), sem("mnat_ready")
        m_sent = [sem(f"m_sent{i}") for i in range(2)]
        st_full, st_free, pv_done, oT_ready = sem("st_full"), sem("st_free"), sem("pv_done"), sem("oT_ready")
        route_ready = sem("route_ready")
        hi_ready, raw_hi, raw_lo = sem("hi_ready"), sem("raw_hi"), sem("raw_lo")
        weights_split = sem("weights_split")
        xb_ready, x2b_ready, h_ready, fin_ready = sem("xb_ready"), sem("x2b_ready"), sem("h_ready"), sem("fin_ready")
        out_done = sem("out_done")
        nat_const = sem("nat_const")
        ps_o_zeroed, kmask_zeroed = sem("ps_o_zeroed"), sem("kmask_zeroed")
        dve_chain, pool_chain = sem("dve_chain"), sem("pool_chain")

        def bg(e):
            return ps_bg[TURN[e] % 2]

        def full(e):
            return TURN[e] + 1

        def emptied(ins, e):
            return ins.then_inc(bg_free[TURN[e] % 2], 1)

        def taken(eng, e):
            eng.wait_ge(bg_free[TURN[e] % 2], TURN[e] // 2 + 1)

        def step(n):
            return n // G, n % G

        def stack_rows(eng, link, which, b):
            in_pairs = lambda w: w[:].rearrange("p t (a two) -> p (t a) two", two=2)
            link(eng.tensor_tensor(in_pairs(rot_c[which]), in_pairs(rot_c[which]),
                                   in_pairs(rot_s[which])[:, :, ::-1], ALU.add))
            if b >= 1:
                eng.wait_ge(bg_full, full(("qs3" if which else "ks3", b - 1)))
            r = rot_c[which][:].rearrange("p t (h d) -> p (t h) d", d=HD)
            rows = nat[which][:].rearrange("p t h r -> p (t h) r")
            at = lambda k: rows[:, :, k * HD:(k + 1) * HD]
            hi, lo, again = (0, 1, 2) if which else (0, 2, 1)
            link(eng.tensor_scalar(at(hi).bitcast(f32r), r, 1.0, 0.0, ALU.mult, ALU.add))
            eng.tensor_scalar(at(again).bitcast(f32r), r, 1.0, 0.0, ALU.mult, ALU.add)
            eng.tensor_tensor(at(lo).bitcast(f32r), r, at(hi), ALU.subtract).then_inc(nat_ready[which], 1)

        block = stack.enter_context(nc.Block())

        @block.sync
        def _(sp):
            xv = x.rearrange("b (t p) d -> p (b t) d", p=P)
            cv = ctx_in.rearrange("b (t p) d -> p (b t) d", p=P)
            by_rows = lambda w: w.rearrange("(k p) n -> p k n", p=P)
            sp.dma_start(c_sb[:, 0:T, :], cv[:, 0:T, :]).then_inc(ld_c[0], 16)
            sp.dma_start(x_sb[:, 0:T, :], xv[:, 0:T, :]).then_inc(ld_x[0], 16)
            sp.dma_start(raw_q[:], by_rows(Wq)).then_inc(ld_wq, 16)
            for b in range(1, B):
                sp.dma_start(c_sb[:, b * T:(b + 1) * T, :], cv[:, b * T:(b + 1) * T, :]).then_inc(ld_c[b], 16)
                sp.dma_start(x_sb[:, b * T:(b + 1) * T, :], xv[:, b * T:(b + 1) * T, :]).then_inc(ld_x[b], 16)
            sp.dma_start(raw_out[:], by_rows(Wout)).then_inc(ld_wout, 16)
            sp.dma_start(raw_up, by_rows(up_w)).then_inc(ld_ffn, 16)
            sp.dma_start(down_sb[:], by_rows(down_w)).then_inc(ld_down, 16)
            sp.dma_start(raw_expert[:, :, 0:D], by_rows(expert_w)).then_inc(ld_ffn, 16)
            sp.dma_start(raw_expert[:, :, D:D + E], by_rows(gate_w)).then_inc(ld_ffn, 16)
            for e in ORDER:
                if e[0] == "KM":
                    b, j = e[1], e[2]
                    groups = slice(2 * j, 2 * j + 2)
                    taken(sp, (f"ks{j}", b))
                    if b == 0:
                        if j < G // 4:
                            sp.wait_ge(kmask_zeroed, 1)
                        else:
                            sp.wait_ge(const_ready, 3)
                    else:
                        sp.wait_ge(st_full, HG * (G * (b - 1) + 2 * j + 2))
                    for i in range(HG):
                        sp.dma_start(kmask[Q * i:Q * (i + 1), groups, i, :].bitcast(f32),
                                     kstack[Q * i:Q * (i + 1), groups, :].bitcast(f32)).then_inc(kmask_ready[j], 16)
                elif e[0] == "MT":
                    m = e[1]
                    b, g = step(2 * m)
                    taken(sp, e)
                    sp.wait_ge(s_full, 8 * (m + 1))
                    for s in range(2):
                        for part in range(2):
                            row = HG * (2 * part + s)
                            sp.dma_start(qstack[b % 2][MROW + part::Q, g + s, :].bitcast(f32),
                                         mT[m % 2][row:row + HG, :].bitcast(f32)).then_inc(m_sent[m % 2], 16)
                elif e[0] == "ln3b":
                    b = e[1]
                    sp.wait_ge(fin_ready, b + 1)
                    sp.dma_start(out[b].rearrange("(t p) d -> p t d", p=P), fin).then_inc(out_done, 16)
            sp.wait_ge(out_done, 16 * B)

        @block.gpsimd
        def _(pool):
            chain = [0]

            def link(ins):
                chain[0] += 1
                ins.then_inc(pool_chain, 1)
                pool.wait_ge(pool_chain, chain[0])

            link(pool.memset(ident[:], 0.0))
            pool.affine_select(out=ident[:], in_=ident[:], compare_op=ALU.not_equal, fill=1.0, base=0,
                               pattern=[[-1, P]], channel_multiplier=1).then_inc(ident_ready, 1)
            link(pool.memset(neg_half[:], -0.5))
            pool.memset(nat[1][:, :, :, MROW:Q], 0.0).then_inc(nat_const, 1)
            pool.memset(nat[0][:, :, :, MROW + 2:Q], 0.0).then_inc(nat_const, 1)
            pool.memset(nat[0][:, :, :, MROW:MROW + 2], 1.0).then_inc(nat_const, 1)
            for i in range(2):
                pool.memset(vaug[i][:, :, :, HD:2 * HD], 1.0).then_inc(const_ready, 1)
            pool.memset(kmask[:, G // 2:G, :, :].bitcast(f32), 0.0).then_inc(const_ready, 1)

            def inverse_deviation(mean_var, plus_eps, result, ready, done, b):
                pool.wait_ge(ready, b + 1)
                link(pool.tensor_scalar(plus_eps[:], mean_var[:, :, 1], EPS, None, ALU.add))
                pool.tensor_tensor(result[:], plus_eps[:], neg_half[:], ALU.pow).then_inc(done, 1)

            pool.wait_ge(raw_hi, 1)
            pool.tensor_tensor(wkv[:, 1, 0, :], raw_kv[:].rearrange("p t d -> p (t d)"), wkv[:, 0, 0, :].bitcast(f32),
                               ALU.subtract).then_inc(raw_lo, 1)
            pool.wait_ge(raw_hi, 2)
            pool.tensor_tensor(wq[:, 1, :, :], raw_q[:], wq[:, 0, :, :].bitcast(f32), ALU.subtract)\
                .then_inc(raw_lo, 1)

            def split_weights(raw, parts):
                pool.wait_ge(ld_wout, 16)
                pool.wait_ge(ld_ffn, 48)
                link(pool.tensor_scalar(parts(0), raw, 1.0, 0.0, ALU.mult, ALU.add))
                pool.tensor_tensor(parts(1), raw, parts(0).bitcast(f32), ALU.subtract).then_inc(weights_split, 1)

            splits = [(raw_out[:], lambda i: wout[:, i, :, :]), (raw_expert, lambda i: expert[:, i, :, :])]
            splits += [(raw_up[:, k, c * 512:(c + 1) * 512], lambda i, k=k, c=c: up[:, i, k, c * 512:(c + 1) * 512])
                       for k in range(KC) for c in range(F // 512)]
            assert len(splits) == WS

            for e in ORDER:
                what, b = e[0], e[1]
                if what == "ln1a":
                    inverse_deviation(mv, var_eps, rstd, mv_ready, rstd_ready, b)
                elif what == "K" and b >= 1:
                    taken(pool, e)
                    stack_rows(pool, link, 0, b)
                elif what == "Q":
                    taken(pool, e)
                    stack_rows(pool, link, 1, b)
                elif what == "o0":
                    if b == 0:
                        pool.wait_ge(ld_vec, 48)
                    pool.wait_ge(xn_ready, b + 1)
                    xv = x_sb[:, b * T:(b + 1) * T, :]
                    pool.tensor_tensor(xv, xv, bout_sb[:].unsqueeze(1).broadcast_to((P, T, D)), ALU.add)\
                        .then_inc(xb_ready, 1)
                elif what == "ln2a":
                    inverse_deviation(mv2, var_eps2, rstd2, mv2_ready, rstd2_ready, b)
                elif what == "x2T":
                    pool.wait_ge(x2n_ready, b + 1)
                    xv = x_sb[:, b * T:(b + 1) * T, :]
                    pool.tensor_tensor(xv, xv, beta_sb[:].unsqueeze(1).broadcast_to((P, T, D)), ALU.add)\
                        .then_inc(x2b_ready, 1)
                elif what == "S" and e[2] == 1 and 1 <= e[1] <= len(splits):
                    split_weights(*splits[e[1] - 1])
                elif what[:2] == "up":
                    j = int(what[2])
                    h = hT[:, 2 * j:2 * j + 2, :]
                    taken(pool, e)
                    pool.tensor_tensor(h, h, h, ALU.mult).then_inc(h_ready, 1)
                elif what == "ln3a":
                    inverse_deviation(mv3, var_eps3, rstd3, mv3_ready, rstd3_ready, b)
                elif what == "ln3b":
                    pool.wait_ge(yn_ready, b + 1)
                    link(pool.tensor_tensor(y, y, gamma_sb[:].unsqueeze(1).broadcast_to((P, T, D)), ALU.mult))
                    pool.wait_ge(x2b_ready, b + 1)
                    if b >= 1:
                        pool.wait_ge(out_done, 16 * b)
                    pool.tensor_tensor(fin, y, x_sb[:, b * T:(b + 1) * T, :], ALU.add).then_inc(fin_ready, 1)

        @block.scalar
        def _(act):
            act.dma_start(pos_sb[:], pos.rearrange("b (t p) a -> p (b t) a", p=P)).then_inc(ld_pos, 16)
            act.dma_start(raw_kv[:].rearrange("p t d -> p (t d)"), Wkv).then_inc(ld_wkv, 16)
            for v, t in ((bout, bout_sb), (gamma, gamma_sb), (beta, beta_sb)):
                act.dma_start(t[:], v.rearrange("(a d) -> a d", a=1).broadcast_to((P, D))).then_inc(ld_vec, 16)
            act.wait_ge(arg_ready, 1)
            act.activation(trig[:], arg[:], ACT.Sin).then_inc(trig_ready, 1)

            act.wait_ge(ld_wkv, 16)
            act.activation(wkv[:, 0, :, :], raw_kv[:].rearrange("p t d -> p (t d)").unsqueeze(1), ACT.Copy)\
                .then_inc(raw_hi, 1)
            act.wait_ge(ld_wq, 16)
            act.activation(wq[:, 0, :, :], raw_q[:], ACT.Copy).then_inc(raw_hi, 1)

            def copy(e, to, of):
                act.wait_ge(bg_full, full(e))
                emptied(act.activation(to, of, ACT.Copy), e)

            def copy_hi(e, to, of):
                act.wait_ge(bg_full, full(e))
                act.activation(to, of, ACT.Copy).then_inc(hi_ready, 1)

            for e in ORDER:
                what, b = e[0], e[1]
                if what == "cT":
                    if b >= 1:
                        act.wait_ge(bg_full, full(("V", b - 1)))
                    copy_hi(e, cT[:, 0, :, :], bg(e)[:, 0:N].unsqueeze(1))
                elif what == "xT":
                    if b >= 1:
                        act.wait_ge(bg_full, full(("Q", b - 1)))
                    copy_hi(e, xnT[:, 0, :, :], bg(e)[:].rearrange("p (k n) -> p k n", k=KC))
                elif what == "V":
                    if b == 0:
                        act.wait_ge(const_ready, 2)
                    if b >= 2:
                        act.wait_ge(pv_done, G * (b - 1))
                    copy(e, vaug[b % 2][:, :, :, 0:HD], bg(e)[:].rearrange("p (t h d) -> p t h d", t=T, h=H))
                elif what[:2] == "ks":
                    j = int(what[2])
                    if b >= 1:
                        act.wait_ge(kmask_ready[j], 64 * b)
                    copy(e, kstack[:, 2 * j:2 * j + 2, :], bg(e)[:].rearrange("p (g n) -> p g n", g=2))
                elif what[:2] == "qs":
                    j = int(what[2])
                    if b >= 2 and j == 0:
                        act.wait_ge(st_full, HG * G * (b - 1))
                    copy(e, qstack[b % 2][:, 2 * j:2 * j + 2, :], bg(e)[:].rearrange("p (g n) -> p g n", g=2))
                elif what == "MT":
                    m = e[1]
                    if m >= 2:
                        act.wait_ge(m_sent[m % 2], 64 * (m // 2))
                    copy(e, mT[m % 2][:], bg(e)[0:4 * HG, 0:N])
                elif what == "ST":
                    n, i = e[1], e[2]
                    k = HG * n + i
                    act.wait_ge(st_full, k + 1)
                    if i == 0 and n >= 2:
                        act.wait_ge(pv_done, n - 1)
                    act.activation(probs[n % 2][:, i, :, :], ps_st[k % 3][:].rearrange("p (t n) -> p t n", t=T),
                                   ACT.Exp, scale=SCALE).then_inc(st_free, 1)
                elif what == "PV":
                    n = e[1]
                    b, g = step(n)
                    act.wait_ge(pv_done, n + 1)
                    if g == 0 and b >= 1:
                        act.wait_ge(bg_full, full(("o3", b - 1)))
                    act.activation(oT[:, g, :], ps_o[:, 0:N], ACT.Copy).then_inc(oT_ready, 1)
                elif what == "aT":
                    if b >= 1:
                        act.wait_ge(bg_full, full(("W", b - 1)))
                    copy_hi(e, attnT[:, 0, :, :], bg(e)[:].rearrange("p (k n) -> p k n", k=KC))
                elif what == "x2T":
                    if b >= 1:
                        act.wait_ge(bg_full, full(("dn", b - 1)))
                    copy_hi(e, x2nT[:, 0, :, :], bg(e)[:].rearrange("p (k n) -> p k n", k=KC))
                elif what[0] == "E":
                    t = int(what[1])
                    act.wait_ge(route_ready, T * b + t + 1)
                    act.wait_ge(bg_full, full(e))
                    if b >= 1:
                        taken(act, ("dn", b - 1))
                    else:
                        act.wait_ge(weights_split, WS)
                    emptied(act.activation(moe[:, t, :], bg(e)[:, 0:D], ACT.Copy, scale=route[:, t:t + 1]), e)
                elif what[:2] == "up":
                    j = int(what[2])
                    act.wait_ge(bg_full, full(e))
                    if j == 0 and b == 0:
                        act.wait_ge(weights_split, WS)
                    elif j == 0:
                        act.wait_ge(bg_full, full(("dn", b - 1)))
                    emptied(act.activation(hT[:, 2 * j:2 * j + 2, :], bg(e)[:].rearrange("p (f n) -> p f n", f=2),
                                           ACT.Relu), e)

        @block.vector
        def _(dve):
            chain = [0]

            def link(ins):
                chain[0] += 1
                ins.then_inc(dve_chain, 1)
                dve.wait_ge(dve_chain, chain[0])

            def mean_variance(source, st, result, ready):
                for t in range(T):
                    ins = dve.bn_stats(st[:, t, :], source[:, t, :])
                link(ins)
                for t in range(T):
                    ins = dve.bn_aggr(result[:, t, :], st[:, t, :])
                ins.then_inc(ready, 1)

            def normalise(to, source, mean_var, r, done):
                for t in range(T):
                    ins = dve.tensor_scalar(to[:, t, :], source[:, t, :], mean_var[:, t, 0:1], r[:, t:t + 1],
                                            ALU.subtract, ALU.mult)
                ins.then_inc(done, 1)

            def rotary_tables():
                dve.wait_ge(ld_pos, 16)
                dve.tensor_copy(ang[:, :, :, 0], pos_sb[:])
                link(dve.tensor_scalar(ang[:, :, :, 1], pos_sb[:], FREQ1, None, ALU.mult))
                a = ang[:].rearrange("p n x f -> p (n x f)")
                magic = 1.5 * 2.0 ** 23
                two_pi = 2 * np.pi
                c1 = float(np.float32(6.28125))
                c2 = float(np.float32(two_pi - c1))
                c3 = float(np.float32(two_pi - c1 - c2))
                pi = float(np.nextafter(np.float32(np.pi), np.float32(0)))
                link(dve.tensor_scalar(turns[:], a, float(1 / two_pi), magic, ALU.mult, ALU.add))
                link(dve.tensor_scalar(turns[:], turns[:], magic, None, ALU.subtract))
                link(dve.scalar_tensor_tensor(out=a, in0=turns[:], scalar=-c1, in1=a, op0=ALU.mult, op1=ALU.add))
                link(dve.scalar_tensor_tensor(out=a, in0=turns[:], scalar=-c2, in1=a, op0=ALU.mult, op1=ALU.add))
                link(dve.scalar_tensor_tensor(out=a, in0=turns[:], scalar=-c3, in1=a, op0=ALU.mult, op1=ALU.add))
                dve.tensor_scalar(arg[:, 0, :], a, pi, -pi, ALU.min, ALU.max)
                link(dve.tensor_scalar(turns[:], a, float(np.pi / 2), None, ALU.add))
                link(dve.tensor_scalar(wrap[:], turns[:], pi, -two_pi, ALU.is_gt, ALU.mult))
                link(dve.tensor_tensor(turns[:], turns[:], wrap[:], ALU.add))
                dve.tensor_scalar(arg[:, 1, :], turns[:], pi, -pi, ALU.min, ALU.max).then_inc(arg_ready, 1)
                dve.wait_ge(trig_ready, 1)
                pairs = lambda t: t[:].rearrange("p n (f two) -> p (n f) two", two=2)
                dve.tensor_copy(pairs(cos8), trig[:, 1, :].unsqueeze(2).broadcast_to((P, 4 * B * T, 2)))
                dve.tensor_copy(pairs(sin8)[:, :, 0], trig[:, 0, :])
                link(dve.tensor_scalar(pairs(sin8)[:, :, 1], trig[:, 0, :], -1.0, None, ALU.mult))

            def rotate(e, which, b):
                dve.wait_ge(bg_full, full(e))
                if b >= 1:
                    dve.wait_ge(nat_ready[which], b)
                elif which:
                    dve.wait_ge(raw_lo, 2)
                source = bg(e)[:].rearrange("p (t h d) -> p t h d", t=T, h=H)
                table = lambda w: w[:, b * T:(b + 1) * T, :].unsqueeze(2).broadcast_to((P, T, H, 8))
                by_head = lambda w: w[:].rearrange("p t (h d) -> p t h d", h=H)
                dve.tensor_tensor(by_head(rot_c[which]), source, table(cos8), ALU.mult)
                emptied(dve.tensor_tensor(by_head(rot_s[which]), source, table(sin8), ALU.mult), e)

            dve.memset(ps_o[:], 0.0).then_inc(ps_o_zeroed, 1)
            dve.memset(kmask[:, 0:G // 2, :, :].bitcast(f32), 0.0).then_inc(kmask_zeroed, 1)
            def lo_part(e, parts, columns):
                dve.wait_ge(hi_ready, SPLIT[e] + 1)
                of = bg(e)[:, 0:columns].rearrange("p (k n) -> p k n", n=N)
                emptied(dve.tensor_tensor(parts[:, 1, :, :], of, parts[:, 0, :, :].bitcast(f32), ALU.subtract), e)

            for e in ORDER:
                what, b = e[0], e[1]
                if what == "cT":
                    if b >= 1:
                        dve.wait_ge(bg_full, full(("V", b - 1)))
                    lo_part(e, cT, N)
                elif what == "xT":
                    if b >= 1:
                        dve.wait_ge(bg_full, full(("Q", b - 1)))
                    lo_part(e, xnT, KC * N)
                elif what == "aT":
                    if b >= 1:
                        dve.wait_ge(bg_full, full(("W", b - 1)))
                    lo_part(e, attnT, KC * N)
                elif what == "x2T":
                    if b >= 1:
                        dve.wait_ge(bg_full, full(("dn", b - 1)))
                    lo_part(e, x2nT, KC * N)
                elif what == "ln1a":
                    dve.wait_ge(ld_x[b], 16)
                    if b >= 1:
                        dve.wait_ge(rstd_ready, b)
                    mean_variance(x_sb[:, b * T:(b + 1) * T, :], stats, mv, mv_ready)
                    if b == 0:
                        rotary_tables()
                elif what == "K":
                    rotate(e, 0, b)
                    if b == 0:
                        taken(dve, e)
                        stack_rows(dve, link, 0, b)
                elif what == "ln1b":
                    dve.wait_ge(rstd_ready, b + 1)
                    if b >= 1:
                        dve.wait_ge(bg_full, full(("xT", b - 1)))
                    normalise(xn, x_sb[:, b * T:(b + 1) * T, :], mv, rstd, xn_ready)
                elif what == "Q":
                    rotate(e, 1, b)
                elif what == "S":
                    n, k = e[1], e[2]
                    m, t, half = n // 2, k // 2, k % 2
                    if k == 0 and n % 2 == 0 and m >= 2:
                        dve.wait_ge(mnat_ready, m - 1)
                        dve.wait_ge(bg_full, full(("MT", m - 2)))
                    dve.wait_ge(s_full, 4 * n + k + 1)
                    dve.tensor_reduce(mneg[m % 2][:, t, n % 2, 2 * half:2 * half + 2],
                                      ps_s[half][:].rearrange("p (i k) -> p i k", i=2),
                                      AX.X, ALU.max, negate=True).then_inc(s_free, 1)
                    if n % 2 and k == 3:
                        dve.wait_ge(s_free, 4 * (n + 1))
                        of = mneg[m % 2][:].rearrange("p t s i -> p t (s i)")
                        hi, lo = (mnat[m % 2][:, :, part, :] for part in range(2))
                        link(dve.tensor_copy(hi.bitcast(f32r), of))
                        dve.tensor_tensor(lo.bitcast(f32r), of, hi, ALU.subtract).then_inc(mnat_ready, 1)
                elif what[0] == "o":
                    t, half = int(what[1]) // 2, int(what[1]) % 2
                    dve.wait_ge(bg_full, full(e))
                    if b >= 1 and what == "o0":
                        dve.wait_ge(bg_full, full(("aT", b - 1)))
                    o = bg(e)[:].rearrange("p (h r) -> p h r", r=Q)
                    r = rden[:, 2 * t + half, :]
                    if b >= 1:
                        taken(dve, (what, b - 1))
                    link(dve.reciprocal(r, o[:, :, HD]))
                    emptied(dve.tensor_tensor(attn[:, t, half * H // 2:(half + 1) * H // 2, :], o[:, :, 0:HD],
                                              r.unsqueeze(2).broadcast_to((P, H // 2, HD)), ALU.mult), e)
                elif what == "W":
                    dve.wait_ge(bg_full, full(e))
                    dve.wait_ge(xb_ready, b + 1)
                    xv = x_sb[:, b * T:(b + 1) * T, :]
                    emptied(dve.tensor_tensor(xv, bg(e)[:].rearrange("p (t d) -> p t d", t=T), xv, ALU.add), e)
                elif what == "ln2a":
                    taken(dve, ("W", b))
                    if b >= 1:
                        dve.wait_ge(rstd2_ready, b)
                    mean_variance(x_sb[:, b * T:(b + 1) * T, :], stats2, mv2, mv2_ready)
                elif what == "ln2b":
                    dve.wait_ge(rstd2_ready, b + 1)
                    if b >= 1:
                        dve.wait_ge(bg_full, full(("x2T", b - 1)))
                    normalise(x2n, x_sb[:, b * T:(b + 1) * T, :], mv2, rstd2, x2n_ready)
                elif what[0] == "E":
                    t = int(what[1])
                    dve.wait_ge(bg_full, full(e))
                    if b >= 1:
                        taken(dve, (what, b - 1))
                    link(dve.max(top8[:, t, :], bg(e)[:, D:D + E]))
                    dve.tensor_tensor(route[:, t:t + 1], top8[:, t, 0:1], top8[:, t, 1:2], ALU.add)\
                        .then_inc(route_ready, 1)
                elif what == "dn":
                    dve.wait_ge(bg_full, full(e))
                    taken(dve, ("E0", b))
                    taken(dve, ("E1", b))
                    if b >= 1:
                        dve.wait_ge(fin_ready, b)
                    else:
                        dve.wait_ge(weights_split, WS)
                    emptied(dve.tensor_tensor(y, bg(e)[:].rearrange("p (t d) -> p t d", t=T), moe[:], ALU.add), e)
                elif what == "ln3a":
                    taken(dve, ("dn", b))
                    if b >= 1:
                        dve.wait_ge(rstd3_ready, b)
                    mean_variance(y, stats3, mv3, mv3_ready)
                elif what == "ln3b":
                    dve.wait_ge(rstd3_ready, b + 1)
                    normalise(y, y, mv3, rstd3, yn_ready)

        @block.tensor
        def _(pe):
            def begin(e):
                k = TURN[e]
                if k >= 2:
                    pe.wait_ge(bg_free[k % 2], k // 2)

            def transposes(e, blocks):
                begin(e)
                at = 0
                for block_ in blocks:
                    m = block_.shape[0]
                    ins = pe.transpose(bg(e)[0:block_.shape[1], at:at + m], block_, ident[:])
                    at += m
                ins.then_inc(bg_full, 1)

            def by_token(e, lhs, rhs, cols):
                begin(e)
                for t in range(T):
                    for k in range(len(rhs)):
                        ins = pe.matmul(bg(e)[:, t * cols:(t + 1) * cols], lhs[k][:, t * P:(t + 1) * P], rhs[k],
                                        start=(k == 0), stop=(k == len(rhs) - 1))
                ins.then_inc(bg_full, 1)

            def split_product(to, lhs, rhs):
                terms = [(k, a, b_) for k in range(len(lhs)) for a, b_ in ((0, 0), (0, 1), (1, 0))]
                for c, (k, a, b_) in enumerate(terms):
                    ins = pe.matmul(to, lhs[k][a], rhs[k][b_], start=(c == 0), stop=(c == len(terms) - 1))
                return ins

            def split_by_token(e, lhs, rhs, kc, cols):
                begin(e)
                for t in range(T):
                    ins = split_product(bg(e)[:, t * D:(t + 1) * D],
                                        [[lhs[:, a, k, t * P:(t + 1) * P] for a in range(2)] for k in range(kc)],
                                        [[rhs[:, a, k, cols] for a in range(2)] for k in range(kc)])
                ins.then_inc(bg_full, 1)

            def tiles(buffer, count):
                return [buffer[:, k, :] for k in range(count)]

            pe.wait_ge(ident_ready, 1)
            for e in ORDER:
                what, b = e[0], e[1]
                if what == "cT":
                    pe.wait_ge(ld_c[b], 16)
                    transposes(e, [c_sb[:, b * T + t, :] for t in range(T)])
                elif what == "K":
                    if b == 0:
                        pe.wait_ge(raw_lo, 1)
                    taken(pe, ("cT", b))
                    split_by_token(e, cT, wkv, 1, slice(0, D))
                elif what == "V":
                    split_by_token(e, cT, wkv, 1, slice(D, 2 * D))
                elif what == "xT":
                    pe.wait_ge(xn_ready, b + 1)
                    transposes(e, [xn[:, t, k * P:(k + 1) * P] for k in range(KC) for t in range(T)])
                elif what == "Q":
                    if b == 0:
                        pe.wait_ge(raw_lo, 2)
                    taken(pe, ("xT", b))
                    split_by_token(e, xnT, wq, KC, slice(0, D))
                elif what[:2] in ("ks", "qs"):
                    which, j = int(what[0] == "q"), int(what[2])
                    if b == 0 and j == 0:
                        pe.wait_ge(nat_const, 3)
                    if j == 0:
                        pe.wait_ge(nat_ready[which], b + 1)
                    rows = nat[which][:].rearrange("p t (g i) r -> p t g (i r)", g=G)
                    transposes(e, [rows[:, t, g, :] for g in (2 * j, 2 * j + 1) for t in range(T)])
                elif what == "S":
                    n, k = e[1], e[2]
                    b, g = step(n)
                    t, half = k // 2, k % 2
                    if g % 2 == 0 and k == 0:
                        pe.wait_ge(kmask_ready[g // 2], 64 * (b + 1))
                        taken(pe, (f"qs{g // 2}", b))
                    if 4 * n + k >= 2:
                        pe.wait_ge(s_free, 4 * n + k - 1)
                    pe.matmul(ps_s[half][:], qstack[b % 2][:, g, t * P:(t + 1) * P],
                              kmask[:, g, 2 * half:2 * half + 2, :], start=True, stop=True).then_inc(s_full, 1)
                elif what == "MT":
                    m = e[1]
                    pe.wait_ge(mnat_ready, m + 1)
                    transposes(e, [mnat[m % 2][:, t, :, :].rearrange("p a i -> p (a i)") for t in range(T)])
                elif what == "ST":
                    n, i = e[1], e[2]
                    b, g = step(n)
                    k = HG * n + i
                    if i == 0 and n % 2 == 0:
                        pe.wait_ge(m_sent[n // 2 % 2], 64 * (n // 4 + 1))
                    if k >= 3:
                        pe.wait_ge(st_free, k - 2)
                    for t in range(T):
                        ins = pe.matmul(ps_st[k % 3][:, t * N:(t + 1) * N], kmask[:, g, i, t * P:(t + 1) * P],
                                        qstack[b % 2][:, g, :], start=True, stop=True)
                    ins.then_inc(st_full, 1)
                elif what == "PV":
                    n = e[1]
                    b, g = step(n)
                    pe.wait_ge(st_free, HG * (n + 1))
                    if n == 0:
                        pe.wait_ge(ps_o_zeroed, 1)
                    else:
                        pe.wait_ge(oT_ready, n)
                    if g == 0:
                        taken(pe, ("V", b))
                    for t in range(T):
                        for i in range(HG):
                            ins = pe.matmul(ps_o[Q * i:Q * i + 2 * HD, 0:N], vaug[b % 2][:, t, HG * g + i, :],
                                            probs[n % 2][:, i, t, :], start=(t == 0), stop=(t == T - 1))
                    ins.then_inc(pv_done, 1)
                elif what[0] == "o":
                    t, half = int(what[1]) // 2, int(what[1]) % 2
                    pe.wait_ge(oT_ready, G * (b + 1))
                    transposes(e, [oT[:, half * G // 2 + j, t * P:(t + 1) * P] for j in range(G // 2)])
                elif what == "aT":
                    taken(pe, ("o3", b))
                    rows = attn[:].rearrange("p t h d -> p t (h d)")
                    transposes(e, [rows[:, t, k * P:(k + 1) * P] for k in range(KC) for t in range(T)])
                elif what == "W":
                    if b == 0:
                        pe.wait_ge(weights_split, WS)
                    taken(pe, ("aT", b))
                    split_by_token(e, attnT, wout, KC, slice(0, D))
                elif what == "x2T":
                    pe.wait_ge(x2n_ready, b + 1)
                    transposes(e, [x2n[:, t, k * P:(k + 1) * P] for k in range(KC) for t in range(T)])
                elif what[0] == "E":
                    t = int(what[1])
                    begin(e)
                    split_product(bg(e)[:, 0:D + E],
                                  [[x2nT[:, a, k, t * P:(t + 1) * P] for a in range(2)] for k in range(KC)],
                                  [[expert[:, a, k, :] for a in range(2)] for k in range(KC)]).then_inc(bg_full, 1)
                elif what[:2] == "up":
                    j = int(what[2])
                    if j == 0:
                        taken(pe, ("x2T", b))
                    begin(e)
                    for f in range(2):
                        tile = slice((2 * j + f) * P, (2 * j + f + 1) * P)
                        ins = split_product(bg(e)[:, f * N:(f + 1) * N],
                                            [[up[:, a, k, tile] for a in range(2)] for k in range(KC)],
                                            [[x2nT[:, a, k, :] for a in range(2)] for k in range(KC)])
                    ins.then_inc(bg_full, 1)
                elif what == "dn":
                    pe.wait_ge(h_ready, 4 * (b + 1))
                    if b == 0:
                        pe.wait_ge(ld_down, 16)
                    by_token(e, tiles(hT, FT), tiles(down_sb, FT), D)


_INS = ["x", "ctx_1024", "fside_BxSx2_0", "L0_xattn_Wq", "L0_xattn_Wkv", "L0_xattn_Wout", "L0_xattn_bout",
        "L0_ffn_gate_w", "L0_ffn_up_w", "L0_ffn_down_w", "L0_ffn_expert_weight", "L0_ffn_ln_gamma",
        "L0_ffn_ln_beta"]


def kernel(**inputs):
    import numpy as _np
    import concourse.bacc as _bacc
    from concourse import mybir as _mybir
    from concourse.bass_utils import run_bass_kernel_spmd as _run

    nc = _bacc.Bacc("TRN2", target_bir_lowering=False, num_devices=1)
    arrays, args = {}, []
    for name in _INS:
        a = _np.ascontiguousarray(inputs[name])
        arrays[f"in_{name}"] = a
        args.append(nc.dram_tensor(f"in_{name}", a.shape, _mybir.dt.from_np(a.dtype), kind="ExternalInput").ap())
    result = nc.dram_tensor("result", inputs["x"].shape, _mybir.dt.float32, kind="ExternalOutput").ap()
    xattn_ffn_kernel(nc, *args, result)
    r = _run(nc, [arrays], core_ids=[0])
    return r.results[0]["result"]
```

```python
import numpy as np
import concourse.bass as bass
from concourse import mybir
from contextlib import ExitStack


BEFORE = {"ln1a": -31, "ln1b": -29.5, "cT": -27.5, "K": -25.5, "xT": -23, "Q": -19.5, "ks0": -15.5,
          "ks1": -14.5, "ks2": -12.5, "V": -11, "ks3": -10, "qs0": -6, "qs1": -3.5, "qs2": -2, "qs3": -1.5}
BEFORE_0 = {"ks2": -6, "qs1": 2, "ks3": 3, "V": 7.5, "qs2": 8, "qs3": 10}
BEFORE_1 = {"ln1a": -25.5, "cT": -19.5, "ln1b": -16.5, "K": -16, "xT": -11, "ks0": -10.5, "Q": -10,
            "ks1": -9, "ks2": -7.5, "ks3": -4.5, "qs0": -3, "qs1": -1, "qs2": 0, "V": 1, "qs3": 1}
AFTER = {"o0": 52, "o1": 52, "aT0": 54.5, "W0": 55.5, "aT1": 56.5, "ln2a0": 57.5, "W1": 58.5,
         "ln2a1": 61.5, "ln2b0": 62, "ln2b1": 62.5, "x2T0": 63.5, "x2T1": 64.5, "E0": 65.5, "up0": 67,
         "E1": 67.5, "h0": 69.5, "up1": 70, "h1": 74, "up2": 74.5, "dn0": 78, "dn1": 78, "h2": 79,
         "up3": 81, "h3": 82, "dn2": 82, "dn3": 84.5, "ln3a0": 84.5, "ln3a1": 87, "ln3b0": 89, "ln3b1": 91}
AFTER_1 = {"o0": 51.5, "o1": 53, "aT0": 53.5, "aT1": 57, "W0": 60, "W1": 60, "ln2a0": 60.5, "ln2a1": 61,
           "ln2b0": 63, "ln2b1": 63, "x2T0": 63.5, "x2T1": 64, "up0": 65.5, "h0": 67, "up1": 69, "h1": 69,
           "up2": 69.5, "E0": 70, "E1": 72, "dn0": 72.5, "h2": 75.5, "up3": 75.5, "dn1": 76.5, "h3": 78.5,
           "dn2": 81, "dn3": 82.5, "ln3a0": 83, "ln3a1": 86.5, "ln3b0": 87, "ln3b1": 94.5}
LAST = {"o0": 147.5, "o1": 149, "aT0": 149, "W0": 150, "aT1": 153, "ln2a0": 155, "ln2b0": 156, "W1": 157.5,
        "ln2a1": 159, "x2T0": 159.5, "ln2b1": 159.5, "E0": 160, "x2T1": 160.5, "up0": 162.5, "up1": 162.5,
        "h0": 163, "E1": 163, "up2": 163.5, "h1": 164, "dn0": 166, "h2": 166, "up3": 166.5, "dn1": 167,
        "h3": 170, "dn2": 171.5, "dn3": 175.5, "ln3a0": 179, "ln3a1": 182, "ln3b0": 183, "ln3b1": 189.5}
BESIDE_LAST = {"aT0": 52.5, "aT1": 56, "W0": 57.5, "ln2a0": 58, "W1": 58, "ln2b0": 58.5, "ln2a1": 59,
               "x2T0": 59.5, "ln2b1": 60, "x2T1": 61.5, "up0": 63, "E0": 65, "h0": 66, "up1": 66, "E1": 68,
               "dn0": 68.5, "h1": 69, "up2": 71.5, "dn1": 71.5, "h2": 73, "up3": 74, "h3": 76.5, "dn2": 80,
               "dn3": 82, "ln3a0": 83, "ln3a1": 85.5, "ln3b0": 92, "ln3b1": 97}
WARM = {"cT": 8, "K": 2, "xT": 4, "Q": 10, "ks0": 15}
WARM_LAST = {"x2T0": 9, "up0": 7}


def order(batches, groups, lag):
    steps, window = batches * groups, 4 * groups
    out = [(w, 0) for w in ("cT", "ln1a", "ln1b", "K", "xT", "Q", "ks0", "ks1")] + [("KM", 0, 1), ("qs0", 0)]
    background = [(at, w, 0) for w, at in BEFORE_0.items()]
    background += [(window + at, w, 1) for w, at in BEFORE_1.items()]
    background += [(window * b + at, w, b) for b in range(2, batches) for w, at in BEFORE.items()]
    background += [(window * b + at, w, b) for b in range(batches - 3) for w, at in AFTER.items()]
    background += [(window * (batches - 3) + at, w, batches - 3) for w, at in AFTER_1.items()]
    background += [(window * (batches - 2) + BESIDE_LAST.get(w, at), w, batches - 2) for w, at in AFTER.items()]
    background += [(at, w, batches - 1) for w, at in LAST.items()]
    background.sort(key=lambda item: item[0])

    for n in range(steps + lag + 2):
        q = n - lag
        for k in range(4):
            if 0 <= q < steps:
                out.append(("ST", q, k))
            if n < steps:
                out.append(("S", n, k))
            if k == 0 and n % 2 == 0 and 2 <= n <= steps:
                out.append(("MT", n // 2 - 1))
            while background and background[0][0] <= 4 * n + k and background[0][0] < 4 * (steps + lag + 1):
                _, w, b = background.pop(0)
                out.append((w, b))
                if b == 0 and w[:2] == "ks":
                    out.append(("KM", 0, int(w[2])))
        if 0 <= q - 1 < steps:
            out.append(("PV", q - 1))
        b, j = divmod(q, groups)
        if j % 2 and 0 <= b < batches - 1:
            out.append(("KM", b + 1, j // 2))
    return out + [(w, b) for _, w, b in background]


def xattn_ffn_kernel(nc, x, ctx_in, pos, Wq, Wkv, Wout, bout, gate_w, up_w, down_w, expert_w,
                     gamma, beta, out):
    f32, f32r = mybir.dt.float32, mybir.dt.float32r
    ALU, ACT, AX = mybir.AluOpType, mybir.ActivationFunctionType, mybir.AxisListType

    P = 128
    B, N, D = x.shape
    CD = ctx_in.shape[2]
    H, HD = 32, 8
    T = N // P
    KC = D // P
    F = up_w.shape[1]
    FT = F // P
    E = gate_w.shape[1]
    HG = 4
    G = H // HG
    Q = P // HG
    EPS = 1e-5
    SCALE = float(1.0 / np.sqrt(np.float32(HD)))
    FREQ1 = float(np.float32(10000.0) ** np.float32(-0.5))
    LAG = 4
    HB = 2
    NS, NST = 2, 2
    UPS = KC * F // 512
    WS = UPS + 2
    MROW = 3 * HD

    ORDER = order(B, G, LAG)
    BANKED = ("cT", "K", "xT", "V", "Q", "ks", "qs", "o", "aT", "W", "x2T", "E", "up", "MT")
    TURN = {}
    for e in ORDER:
        if e[0].rstrip("0123") in BANKED or e[0] in BANKED:
            TURN[e] = len(TURN)
    SPLIT = {e: k for k, e in enumerate(e for e in ORDER if e[0].rstrip("01") in ("cT", "xT", "aT", "x2T"))}

    def by_token_uses(t):
        return [e for e in ORDER if e[0] in ("ln1b", "xT", f"o{t}", f"aT{t}", f"ln2b{t}", f"x2T{t}")]

    for t in range(T):
        uses = by_token_uses(t)
        assert all(w[1] == r[1] and (w[0][:2], r[0][:2]) in (("ln", "xT"), ("o" + str(t), "aT"), ("ln", "x2"))
                   for w, r in zip(uses[::2], uses[1::2])), "uses of the buffer in turn"

    with ExitStack() as stack:
        def sb(name, shape, dt=f32):
            return stack.enter_context(nc.sbuf_tensor(name, shape, dt))

        def bank(name):
            return stack.enter_context(nc.psum_tensor(name, [P, 512], f32))

        def sem(name):
            return stack.enter_context(nc.semaphore(name))

        x_sb = sb("x_sb", [P, B * T, D])
        c_sb = sb("c_sb", [P, 2 * T, CD])
        pos_sb = sb("pos_sb", [P, B * T, 2])
        wq = sb("wq", [P, 2, KC, D], f32r)
        wkv = sb("wkv", [P, 2, 1, 2 * D], f32r)
        wout = sb("wout", [P, 2, KC, D], f32r)
        up = sb("up", [P, 2, KC, F], f32r)
        expert = sb("expert", [P, 2, KC, D + E], f32r)
        down = sb("down", [P, 2, FT, D], f32r)
        bout_sb = sb("bout_sb", [P, D])
        gamma_sb = sb("gamma_sb", [P, D])
        beta_sb = sb("beta_sb", [P, D])
        ident = sb("ident", [P, P])
        neg_half = sb("neg_half", [P, T])
        table_probe = sb("table_probe", [P, T])
        cos8 = sb("cos8", [P, B * T, 8])
        sin8 = sb("sin8", [P, B * T, 8])
        stats = sb("stats", [P, T, 6])
        mv = sb("mv", [P, T, 2])
        var_eps = sb("var_eps", [P, T])
        rstd = sb("rstd", [P, T])
        xn = sb("by_token", [P, T, D])
        xnT = sb("xnT", [P, 2, KC, N], f32r)
        cT = sb("cT", [P, 2, 1, N], f32r)
        rot_c = sb("rot_c", [P, T, D])
        rot_s = sb("rot_s", [P, T, D])
        nat = [sb(f"nat{i}", [P, T, H, Q]) for i in range(2)]
        kstack = sb("kstack", [P, G, N], f32r)
        kmask = sb("kmask", [P, G, HG, N], f32r)
        qstack = [sb(f"qstack{i}", [P, G, N], f32r) for i in range(2)]
        vaug = [sb(f"vaug{i}", [P, T, H // 2, 6 * HD]) for i in range(2)]
        mneg = [sb(f"mneg{i}", [P, T, 2, HG]) for i in range(2)]
        mnat = [sb(f"mnat{i}", [P, T, 2, HG * 2]) for i in range(2)]
        mT = [sb(f"mT{i}", [2 * HG * 2, N], f32r) for i in range(2)]
        probs = [sb(f"probs{i}", [P, HG, T, N]) for i in range(2)]
        oT = sb("oT", [P, G // 2, N])
        rden = sb("rden", [P, T, H])
        attn = xn[:].rearrange("p t (h d) -> p t h d", h=H)
        attnT = sb("attnT", [P, 2, KC, N], f32r)
        stats2 = sb("stats2", [P, T, 6])
        mv2 = sb("mv2", [P, T, 2])
        var_eps2 = sb("var_eps2", [P, T])
        rstd2 = sb("rstd2", [P, T])
        x2n = xn
        x2nT = sb("x2nT", [P, 2, KC, N], f32r)
        top8 = sb("top8", [P, T, 8])
        route = sb("route", [P, T])
        moe = sb("moe", [P, T, D])
        y_fin = sb("y_fin", [P, 2 * T * D])
        y, fin = (y_fin[:, i * T * D:(i + 1) * T * D].rearrange("p (t d) -> p t d", t=T) for i in range(2))
        whole = [sb(f"whole{i}", [P, 2, N]) for i in range(HB)]
        inner = sb("inner", [P, 2, 2, 2, N], f32r)
        raw_up = [oT[:].rearrange("p g n -> p (g n)"), y_fin[:]]
        raw_q, raw_kv = (probs[0][:, i:i + 2, :, :].rearrange("p i t n -> p (i t n)") for i in (0, 2))
        raw_q = raw_q[:, 0:KC * D].rearrange("p (k n) -> p k n", k=KC)
        raw_kv = raw_kv[:, 0:2 * D]
        raw_out = moe
        raw_expert = y_fin[:, 0:KC * (D + E)].rearrange("p (k n) -> p k n", k=KC)
        A = 4 * B * T
        scratch = probs[1][:].rearrange("p i t n -> p (i t n)")
        ang, turns, wrap = (scratch[:, i * A:(i + 1) * A] for i in range(3))
        arg = scratch[:, 3 * A:5 * A].rearrange("p (s a) -> p s a", s=2)
        trig = scratch[:, 5 * A:7 * A].rearrange("p (s a) -> p s a", s=2)
        stats3 = sb("stats3", [P, T, 6])
        mv3 = sb("mv3", [P, T, 2])
        var_eps3 = sb("var_eps3", [P, T])
        rstd3 = sb("rstd3", [P, T])

        ps_s = [bank(f"ps_s{i}") for i in range(NS)]
        ps_st = [bank(f"ps_st{i}") for i in range(NST)]
        ps_o = bank("ps_o")
        ps_bg = [bank(f"ps_bg{i}") for i in range(2)]
        ps_dn = bank("ps_dn")

        ld_x = [sem(f"ld_x{b}") for b in range(B)]
        ld_c = [sem(f"ld_c{b}") for b in range(B)]
        ld_down = [sem(f"ld_down{i}") for i in range(HB)]
        ld_pos, ld_wq, ld_wkv, ld_vec = (sem(s) for s in ("ld_pos", "ld_wq", "ld_wkv", "ld_vec"))
        ld_up, ld_wout, ld_expert = sem("ld_up"), sem("ld_wout"), sem("ld_expert")
        ident_ready, const_ready = sem("ident_ready"), sem("const_ready")
        arg_ready, trig_ready = sem("arg_ready"), sem("trig_ready")
        tables_ready = sem("tables_ready")
        rotated_ready, second_hi = sem("rotated_ready"), sem("second_hi")
        mv_ready, rstd_ready, xn_ready = sem("mv_ready"), sem("rstd_ready"), sem("xn_ready")
        mv2_ready, rstd2_ready, x2n_ready = sem("mv2_ready"), sem("rstd2_ready"), sem("x2n_ready")
        mv3_ready, rstd3_ready, yn_ready = sem("mv3_ready"), sem("rstd3_ready"), sem("yn_ready")
        bg_full = sem("bg_full")
        bg_free = [sem(f"bg_free{i}") for i in range(2)]
        nat_ready = [sem(f"nat_ready{i}") for i in range(2)]
        kmask_ready = [sem(f"kmask_ready{j}") for j in range(G // 2)]
        s_full, s_free, mnat_ready = sem("s_full"), sem("s_free"), sem("mnat_ready")
        m_sent = [sem(f"m_sent{i}") for i in range(2)]
        st_full, st_free, pv_done, oT_ready = sem("st_full"), sem("st_free"), sem("pv_done"), sem("oT_ready")
        route_ready = sem("route_ready")
        hi_ready, raw_hi, raw_lo = sem("hi_ready"), sem("raw_hi"), sem("raw_lo")
        piece_hi, weights_split = sem("piece_hi"), sem("weights_split")
        xb_ready, x2b_ready, fin_ready = sem("xb_ready"), sem("x2b_ready"), sem("fin_ready")
        square_ready, h_hi_ready, h_ready = sem("square_ready"), sem("h_hi_ready"), sem("h_ready")
        dn_read, dn_full, y_ready, down_split = sem("dn_read"), sem("dn_full"), sem("y_ready"), sem("down_split")
        out_done = [sem(f"out_done{t}") for t in range(T)]
        nat_const = sem("nat_const")
        kmask_zeroed = sem("kmask_zeroed")
        dve_chain, pool_chain = sem("dve_chain"), sem("pool_chain")

        def bg(e):
            return ps_bg[TURN[e] % 2]

        def full(e):
            return TURN[e] + 1

        def bg_read(eng, *entries):
            eng.wait_ge(bg_full, max(full(e) for e in entries))

        def emptied(ins, e):
            return ins.then_inc(bg_free[TURN[e] % 2], 1)

        def taken(eng, e):
            eng.wait_ge(bg_free[TURN[e] % 2], TURN[e] // 2 + 1)

        def sent(j, b):
            return 16 * HG * (b + (j > 0))

        def step(n):
            return n // G, n % G

        def stack_rows(eng, link, which, b):
            in_pairs = lambda w: w[:].rearrange("p t (a two) -> p (t a) two", two=2)
            rotated = eng.tensor_tensor(in_pairs(rot_c), in_pairs(rot_c),
                                        in_pairs(rot_s)[:, :, ::-1], ALU.add)
            if b >= 1:
                link(rotated)
            else:
                rotated.then_inc(rotated_ready, 1)
                eng.wait_ge(rotated_ready, which + 1)
            if b >= 1:
                eng.wait_ge(bg_full, full(("qs3" if which else "ks3", b - 1)))
            r = rot_c[:].rearrange("p t (h d) -> p (t h) d", d=HD)
            rows = nat[which][:].rearrange("p t h r -> p (t h) r")
            at = lambda k: rows[:, :, k * HD:(k + 1) * HD]
            hi, lo, again = (0, 1, 2) if which else (0, 2, 1)
            link(eng.tensor_scalar(at(hi).bitcast(f32r), r, 1.0, 0.0, ALU.mult, ALU.add))
            if b >= 1:
                eng.tensor_scalar(at(again).bitcast(f32r), r, 1.0, 0.0, ALU.mult, ALU.add)
            eng.tensor_tensor(at(lo).bitcast(f32r), r, at(hi), ALU.subtract).then_inc(nat_ready[which], 1)

        def squares(eng, e, j):
            h = whole[j % HB][:]
            if e == ("up0", B - 1):
                eng.wait_ge(h_ready, 4 * (B - 1))
            taken(eng, e)
            eng.tensor_tensor(h, h, h, ALU.mult).then_inc(square_ready, 1)

        def lo_squares(eng, b, j):
            k = 4 * b + j
            eng.wait_ge(square_ready, k + 1)
            eng.wait_ge(h_hi_ready, k + 1)
            hi, lo = (inner[:, j % 2, part, :, :] for part in range(2))
            inner_read(eng, b, j)
            eng.tensor_tensor(lo, whole[j % HB][:], hi.bitcast(f32), ALU.subtract).then_inc(h_ready, 1)

        def inner_read(eng, b, j):
            if j >= 2:
                eng.wait_ge(dn_read, 3 * b + j - 1)
            elif b >= 1 and j == 0:
                eng.wait_ge(dn_read, 3 * b)
            elif b >= 1:
                eng.wait_ge(dn_full, b)

        PIECES = [(raw_up[k][:, c * 512:(c + 1) * 512], lambda i, k=k, c=c: up[:, i, k, c * 512:(c + 1) * 512],
                   (ld_up, 32), weights_split) for k in range(KC) for c in range(F // 512)]
        PIECES += [(raw_out[:], lambda i: wout[:, i, :, :], (ld_wout, 16), weights_split)]
        PIECES += [(whole[j % HB][:], lambda i, j=j: down[:, i, 2 * j:2 * j + 2, :],
                    (ld_down[j % HB], 16 * (j // HB + 1)), down_split) for j in range(FT // 2)]
        PIECES += [(raw_expert, lambda i: expert[:, i, :, :], (ld_expert, 32), weights_split)]

        def piece_at(e):
            if e[0] == "S" and e[2] % 2 and 2 * e[1] + e[2] // 2 < len(PIECES):
                return 2 * e[1] + e[2] // 2

        block = stack.enter_context(nc.Block())

        @block.sync
        def _(sp):
            xv = x.rearrange("b (t p) d -> p (b t) d", p=P)
            cv = ctx_in.rearrange("b (t p) d -> p (b t) d", p=P)
            by_rows = lambda w: w.rearrange("(k p) n -> p k n", p=P)

            def load_context(b):
                ring = slice(b % 2 * T, (b % 2 + 1) * T)
                sp.dma_start(c_sb[:, ring, :], cv[:, b * T:(b + 1) * T, :]).then_inc(ld_c[b], 16)

            def load_down(j):
                sp.dma_start(whole[j % HB][:], by_rows(down_w)[:, 2 * j:2 * j + 2, :]).then_inc(ld_down[j % HB], 16)

            def load_tokens(b):
                tiles = slice(b * T, (b + 1) * T)
                if b < 2:
                    load_context(b)
                if b == 0:
                    sp.dma_start(raw_kv, Wkv).then_inc(ld_wkv, 16)
                sp.dma_start(x_sb[:, tiles, :], xv[:, tiles, :]).then_inc(ld_x[b], 16)

            load_tokens(0)
            sp.dma_start(raw_q, by_rows(Wq)).then_inc(ld_wq, 16)
            load_tokens(1)
            for k in range(KC):
                sp.dma_start(raw_up[k], up_w[k * P:(k + 1) * P, :]).then_inc(ld_up, 16)
            sp.dma_start(raw_out[:], by_rows(Wout)).then_inc(ld_wout, 16)
            for j in range(HB):
                load_down(j)
            for b in range(2, B):
                load_tokens(b)
            for v, t in ((bout, bout_sb), (gamma, gamma_sb), (beta, beta_sb)):
                sp.dma_start(t[:], v.rearrange("(a d) -> a d", a=1).broadcast_to((P, D))).then_inc(ld_vec, 16)
            downs = HB
            for e in ORDER:
                if e == ("S", 3, 0):
                    sp.wait_ge(weights_split, UPS)
                    sp.dma_start(raw_expert[:, :, 0:D], by_rows(expert_w)).then_inc(ld_expert, 16)
                    sp.dma_start(raw_expert[:, :, D:D + E], by_rows(gate_w)).then_inc(ld_expert, 16)
                if e[0] == "S" and e[2] == 0 and 2 * e[1] > UPS + 1 + downs - HB and downs < FT // 2:
                    sp.wait_ge(down_split, downs - HB + 1)
                    load_down(downs)
                    downs += 1
                if e[0] == "V" and e[1] + 2 < B:
                    sp.wait_ge(bg_full, full(("cT", e[1])))
                    load_context(e[1] + 2)
                if e[0] == "KM":
                    b, j = e[1], e[2]
                    groups = slice(2 * j, 2 * j + 2)
                    taken(sp, (f"ks{j}", b))
                    if b == 0:
                        sp.wait_ge(const_ready, j)
                    else:
                        sp.wait_ge(st_full, HG * (G * (b - 1) + 2 * j + 2))
                    for i in range(HG):
                        sp.dma_start(kmask[Q * i:Q * (i + 1), groups, i, :].bitcast(f32),
                                     kstack[Q * i:Q * (i + 1), groups, :].bitcast(f32)).then_inc(kmask_ready[j], 16)
                elif e[0] == "MT":
                    m = e[1]
                    b, g = step(2 * m)
                    taken(sp, e)
                    sp.wait_ge(s_full, 8 * (m + 1))
                    for s in range(2):
                        for part in range(2):
                            row = HG * (2 * part + s)
                            sp.dma_start(qstack[b % 2][MROW + part::Q, g + s, :].bitcast(f32),
                                         mT[m % 2][row:row + HG, :].bitcast(f32)).then_inc(m_sent[m % 2], 16)
                elif e[0][:4] == "ln3b":
                    b, t = e[1], int(e[0][4])
                    sp.wait_ge(fin_ready, T * b + t + 1)
                    sp.dma_start(out[b, t * P:(t + 1) * P, :], fin[:, t, :]).then_inc(out_done[t], 16)
            for t in range(T):
                sp.wait_ge(out_done[t], 16 * B)

        @block.gpsimd
        def _(pool):
            chain = [0]

            def link(ins):
                chain[0] += 1
                ins.then_inc(pool_chain, 1)
                pool.wait_ge(pool_chain, chain[0])

            link(pool.memset(ident[:], 0.0))
            pool.affine_select(out=ident[:], in_=ident[:], compare_op=ALU.not_equal, fill=1.0, base=0,
                               pattern=[[-1, P]], channel_multiplier=1).then_inc(ident_ready, 1)
            link(pool.memset(neg_half[:], -0.5))
            pool.memset(nat[0][:, :, :, MROW + 2:Q], 0.0).then_inc(nat_const, 1)
            pool.memset(nat[0][:, :, :, MROW:MROW + 2], 1.0).then_inc(nat_const, 1)
            pool.memset(nat[1][:, :, :, MROW:Q], 0.0).then_inc(nat_const, 1)
            pool.memset(kmask[:, 2:4, :, :].bitcast(f32), 0.0).then_inc(const_ready, 1)

            def inverse_deviation(mean_var, plus_eps, result, ready, done, count):
                pool.wait_ge(ready, count + 1)
                link(pool.tensor_scalar(plus_eps, mean_var[:, :, 1], EPS, None, ALU.add))
                pool.tensor_tensor(result, plus_eps, neg_half[:, 0:result.shape[1]], ALU.pow).then_inc(done, 1)

            for e in ORDER:
                what, b = e[0], e[1]
                if what == "ln1a":
                    if b == 0:
                        pool.wait_ge(raw_hi, 1)
                        pool.tensor_tensor(wkv[:, 1, 0, :], raw_kv,
                                           wkv[:, 0, 0, :].bitcast(f32), ALU.subtract).then_inc(raw_lo, 1)
                    inverse_deviation(mv[:], var_eps[:], rstd[:], mv_ready, rstd_ready, b)
                    if b == 0:
                        pool.wait_ge(raw_hi, 2)
                        pool.tensor_tensor(wq[:, 1, :, :], raw_q, wq[:, 0, :, :].bitcast(f32), ALU.subtract)\
                            .then_inc(raw_lo, 1)
                        pool.memset(kmask[:, 4:6, :, :].bitcast(f32), 0.0).then_inc(const_ready, 1)
                elif what in ("K", "Q"):
                    which = int(what == "Q")
                    if b >= 1:
                        taken(pool, e)
                        stack_rows(pool, link, which, b)
                    else:
                        pool.wait_ge(rotated_ready, which + 1)
                        rows = nat[which][:].rearrange("p t h r -> p (t h) r")
                        again = 2 if which else 1
                        pool.tensor_scalar(rows[:, :, again * HD:(again + 1) * HD].bitcast(f32r),
                                           rot_c[:].rearrange("p t (h d) -> p (t h) d", d=HD),
                                           1.0, 0.0, ALU.mult, ALU.add).then_inc(second_hi, 1)
                        if which == 0:
                            pool.memset(kmask[:, 6:8, :, :].bitcast(f32), 0.0).then_inc(const_ready, 1)
                            for i in range(2):
                                parts = vaug[i][:].rearrange("p t h (c r) -> p t h c r", c=3)
                                pool.memset(parts[:, :, :, 1, :], 0.0).then_inc(const_ready, 1)
                                for c in (0, 2):
                                    pool.memset(parts[:, :, :, c, HD:2 * HD], 1.0).then_inc(const_ready, 1)
                elif what == "o0":
                    if b == 0:
                        pool.wait_ge(ld_vec, 48)
                    pool.wait_ge(xn_ready, b + 1)
                    xv = x_sb[:, b * T:(b + 1) * T, :]
                    pool.tensor_tensor(xv, xv, bout_sb[:].unsqueeze(1).broadcast_to((P, T, D)), ALU.add)\
                        .then_inc(xb_ready, 1)
                elif what[:4] == "ln2a":
                    t = int(what[4])
                    inverse_deviation(mv2[:, t:t + 1, :], var_eps2[:, t:t + 1], rstd2[:, t:t + 1],
                                      mv2_ready, rstd2_ready, T * b + t)
                elif what == "x2T1":
                    pool.wait_ge(x2n_ready, T * (b + 1))
                    xv = x_sb[:, b * T:(b + 1) * T, :]
                    pool.tensor_tensor(xv, xv, beta_sb[:].unsqueeze(1).broadcast_to((P, T, D)), ALU.add)\
                        .then_inc(x2b_ready, 1)
                elif piece_at(e) is not None:
                    i = piece_at(e)
                    raw, parts, _, done = PIECES[i]
                    pool.wait_ge(piece_hi, i + 1)
                    pool.tensor_tensor(parts(1), raw, parts(0).bitcast(f32), ALU.subtract)\
                        .then_inc(done, 1)
                elif what[:2] == "up":
                    j = int(what[2])
                    if b < B - 1:
                        squares(pool, e, j)
                elif what[0] == "h":
                    if b < B - 1:
                        lo_squares(pool, b, int(what[1]))
                elif what[:4] == "ln3a":
                    t = int(what[4])
                    inverse_deviation(mv3[:, t:t + 1, :], var_eps3[:, t:t + 1], rstd3[:, t:t + 1],
                                      mv3_ready, rstd3_ready, T * b + t)

        @block.scalar
        def _(act):
            act.dma_start(pos_sb[:], pos.rearrange("b (t p) a -> p (b t) a", p=P)).then_inc(ld_pos, 16)

            act.wait_ge(pool_chain, 2)
            act.activation(table_probe[:], neg_half[:], ACT.Sin)

            def sines():
                act.wait_ge(arg_ready, 1)
                act.activation(trig, arg, ACT.Sin).then_inc(trig_ready, 1)

            def first_weights():
                act.wait_ge(ld_wkv, 16)
                act.activation(wkv[:, 0, :, :], raw_kv.unsqueeze(1), ACT.Copy)\
                    .then_inc(raw_hi, 1)
                sines()
                act.wait_ge(ld_wq, 16)
                act.activation(wq[:, 0, :, :], raw_q, ACT.Copy).then_inc(raw_hi, 1)

            def copy(e, to, of):
                act.wait_ge(bg_full, full(e))
                emptied(act.activation(to, of, ACT.Copy), e)

            def copy_hi(e, to, of):
                act.wait_ge(bg_full, full(e))
                act.activation(to, of, ACT.Copy).then_inc(hi_ready, 1)

            for e in ORDER:
                what, b = e[0], e[1]
                if piece_at(e) is not None:
                    raw, parts, load, _ = PIECES[piece_at(e)]
                    act.wait_ge(*load)
                    act.activation(parts(0), raw, ACT.Copy).then_inc(piece_hi, 1)
                if what == "cT":
                    if b >= 1:
                        act.wait_ge(bg_full, full(("V", b - 1)))
                    copy_hi(e, cT[:, 0, :, :], bg(e)[:, 0:N].unsqueeze(1))
                    if b == 0:
                        first_weights()
                elif what == "xT":
                    if b >= 1:
                        act.wait_ge(bg_full, full(("Q", b - 1)))
                    copy_hi(e, xnT[:, 0, :, :], bg(e)[:].rearrange("p (k n) -> p k n", k=KC))
                elif what == "V":
                    if b == 0:
                        act.wait_ge(const_ready, G // 2 - 1 + 6)
                    if b >= 2:
                        act.wait_ge(pv_done, G * (b - 1))
                    act.wait_ge(bg_full, full(e))
                    for s in range(2):
                        to = vaug[b % 2][:].rearrange("p t (m i) (c r) -> p (t m) i c r", i=HG, c=3)[:, :, :, 2 * s, 0:HD]
                        of = bg(e)[:].rearrange("p (m s i d) -> p m s i d", s=2, i=HG, d=HD)[:, :, s, :, :]
                        ins = act.activation(to, of, ACT.Copy)
                    emptied(ins, e)
                elif what[:2] == "ks":
                    j = int(what[2])
                    if b >= 1 and sent(j, b - 1):
                        act.wait_ge(kmask_ready[j], sent(j, b - 1))
                    if (b, j) == (0, 0):
                        act.wait_ge(bg_full, full(e))
                        act.wait_ge(kmask_zeroed, 1)
                        for i in range(HG):
                            rows = slice(Q * i, Q * (i + 1))
                            ins = act.activation(kmask[rows, 0:2, i, :], bg(e)[rows, :].rearrange("p (g n) -> p g n", g=2),
                                                 ACT.Copy)
                        emptied(ins, e)
                    else:
                        copy(e, kstack[:, 2 * j:2 * j + 2, :], bg(e)[:].rearrange("p (g n) -> p g n", g=2))
                elif what[:2] == "qs":
                    j = int(what[2])
                    if b >= 2 and j == 0:
                        act.wait_ge(st_full, HG * G * (b - 1))
                    copy(e, qstack[b % 2][:, 2 * j:2 * j + 2, :], bg(e)[:].rearrange("p (g n) -> p g n", g=2))
                    if e == ("qs0", 0):
                        act.activation(table_probe[:], neg_half[:], ACT.Exp)
                elif what == "MT":
                    m = e[1]
                    if m >= 2:
                        act.wait_ge(m_sent[m % 2], 64 * (m // 2))
                    copy(e, mT[m % 2][:], bg(e)[0:4 * HG, 0:N])
                elif what == "ST":
                    n, i = e[1], e[2]
                    k = HG * n + i
                    act.wait_ge(st_full, k + 1)
                    if i == 0 and n >= 2:
                        act.wait_ge(pv_done, n - 1)
                    elif i == 0:
                        act.wait_ge(raw_lo, 2)
                        act.wait_ge(tables_ready, 1)
                    act.activation(probs[n % 2][:, i, :, :], ps_st[k % NST][:].rearrange("p (t n) -> p t n", t=T),
                                   ACT.Exp, scale=SCALE).then_inc(st_free, 1)
                elif what == "PV":
                    n = e[1]
                    b, g = step(n)
                    if g % 2:
                        act.wait_ge(pv_done, n + 1)
                        if g == 1 and b >= 1:
                            bg_read(act, ("o1", b - 1))
                        elif g == 1:
                            act.wait_ge(weights_split, UPS)
                        act.activation(oT[:, g // 2, :], ps_o[:, 0:N], ACT.Copy).then_inc(oT_ready, 1)
                elif what[:2] == "aT":
                    t = int(what[2])
                    if b >= 1:
                        bg_read(act, (f"W{t}", b - 1))
                    copy_hi(e, attnT[:, 0, :, t * P:(t + 1) * P], bg(e)[:, 0:D].rearrange("p (k n) -> p k n", k=KC))
                elif what[:3] == "x2T":
                    t = int(what[3])
                    if b >= 1:
                        bg_read(act, ("E1", b - 1), ("up3", b - 1))
                    copy_hi(e, x2nT[:, 0, :, t * P:(t + 1) * P], bg(e)[:, 0:D].rearrange("p (k n) -> p k n", k=KC))
                elif what[0] == "E":
                    t = int(what[1])
                    act.wait_ge(route_ready, T * b + t + 1)
                    act.wait_ge(bg_full, full(e))
                    if b >= 1:
                        act.wait_ge(y_ready, T * (b - 1) + t + 1)
                    else:
                        act.wait_ge(weights_split, WS)
                    emptied(act.activation(moe[:, t, :], bg(e)[:, 0:D], ACT.Copy, scale=route[:, t:t + 1]), e)
                elif what[:2] == "up":
                    j = int(what[2])
                    act.wait_ge(bg_full, full(e))
                    if 4 * b + j >= HB:
                        act.wait_ge(h_ready, 4 * b + j - HB + 1)
                    else:
                        act.wait_ge(down_split, FT // 2)
                    emptied(act.activation(whole[j % HB][:],
                                           bg(e)[:].rearrange("p (f n) -> p f n", f=2), ACT.Relu), e)
                elif what[0] == "h":
                    j = int(what[1])
                    act.wait_ge(square_ready, 4 * b + j + 1)
                    inner_read(act, b, j)
                    act.activation(inner[:, j % 2, 0, :, :], whole[j % HB][:], ACT.Copy)\
                        .then_inc(h_hi_ready, 1)

        @block.vector
        def _(dve):
            chain = [0]

            def link(ins):
                chain[0] += 1
                ins.then_inc(dve_chain, 1)
                dve.wait_ge(dve_chain, chain[0])

            def mean_variance(source, st, result, ready):
                for t in range(source.shape[1]):
                    ins = dve.bn_stats(st[:, t, :], source[:, t, :])
                link(ins)
                for t in range(source.shape[1]):
                    ins = dve.bn_aggr(result[:, t, :], st[:, t, :])
                ins.then_inc(ready, 1)

            def normalise(to, source, mean_var, r, done):
                for t in range(source.shape[1]):
                    ins = dve.tensor_scalar(to[:, t, :], source[:, t, :], mean_var[:, t, 0:1], r[:, t:t + 1],
                                            ALU.subtract, ALU.mult)
                ins.then_inc(done, 1)

            def angles_in_turns():
                dve.wait_ge(ld_pos, 16)
                a = ang
                by_frequency = a.rearrange("p (n x f) -> p n x f", n=B * T, f=2)
                dve.tensor_copy(by_frequency[:, :, :, 0], pos_sb[:])
                link(dve.tensor_scalar(by_frequency[:, :, :, 1], pos_sb[:], FREQ1, None, ALU.mult))
                two_pi = 2 * np.pi
                magic = 1.5 * 2.0 ** 23
                link(dve.tensor_scalar(turns, a, float(1 / two_pi), magic, ALU.mult, ALU.add))
                link(dve.tensor_scalar(turns, turns, magic, None, ALU.subtract))

            def rotary_angles():
                a = ang
                two_pi = 2 * np.pi
                c1 = float(np.float32(6.28125))
                c2 = float(np.float32(two_pi - c1))
                c3 = float(np.float32(two_pi - c1 - c2))
                pi = float(np.nextafter(np.float32(np.pi), np.float32(0)))
                link(dve.scalar_tensor_tensor(out=a, in0=turns, scalar=-c1, in1=a, op0=ALU.mult, op1=ALU.add))
                link(dve.scalar_tensor_tensor(out=a, in0=turns, scalar=-c2, in1=a, op0=ALU.mult, op1=ALU.add))
                link(dve.scalar_tensor_tensor(out=a, in0=turns, scalar=-c3, in1=a, op0=ALU.mult, op1=ALU.add))
                dve.tensor_scalar(arg[:, 0, :], a, pi, -pi, ALU.min, ALU.max)
                link(dve.tensor_scalar(turns, a, float(np.pi / 2), None, ALU.add))
                link(dve.tensor_scalar(wrap, turns, pi, -two_pi, ALU.is_gt, ALU.mult))
                link(dve.tensor_tensor(turns, turns, wrap, ALU.add))
                dve.tensor_scalar(arg[:, 1, :], turns, pi, -pi, ALU.min, ALU.max).then_inc(arg_ready, 1)

            def rotary_tables():
                dve.wait_ge(trig_ready, 1)
                pairs = lambda t: t[:].rearrange("p n (f two) -> p (n f) two", two=2)
                dve.tensor_copy(pairs(cos8), trig[:, 1, :].unsqueeze(2).broadcast_to((P, 4 * B * T, 2)))
                dve.tensor_copy(pairs(sin8)[:, :, 0], trig[:, 0, :])
                dve.tensor_scalar(pairs(sin8)[:, :, 1], trig[:, 0, :], -1.0, None, ALU.mult).then_inc(tables_ready, 1)
                dve.wait_ge(tables_ready, 1)

            def rotate(e, which, b):
                dve.wait_ge(bg_full, full(e))
                if which:
                    dve.wait_ge(nat_ready[0], b + 1)
                    if b == 0:
                        dve.wait_ge(second_hi, 1)
                elif b >= 1:
                    dve.wait_ge(nat_ready[1], b)
                    if b == 1:
                        dve.wait_ge(second_hi, 2)
                source = bg(e)[:].rearrange("p (t h d) -> p t h d", t=T, h=H)
                table = lambda w: w[:, b * T:(b + 1) * T, :].unsqueeze(2).broadcast_to((P, T, H, 8))
                by_head = lambda w: w[:].rearrange("p t (h d) -> p t h d", h=H)
                dve.tensor_tensor(by_head(rot_c), source, table(cos8), ALU.mult)
                emptied(dve.tensor_tensor(by_head(rot_s), source, table(sin8), ALU.mult), e)

            dve.memset(kmask[:, 0:2, :, :].bitcast(f32), 0.0).then_inc(kmask_zeroed, 1)

            def by_token_read(e):
                before = [by_token_uses(t)[by_token_uses(t).index(e) - 1] for t in range(T) if e in by_token_uses(t)]
                bg_read(dve, *before)

            def lo_part(e, parts, tokens=slice(0, N)):
                hi, lo = (parts[:, part, :, tokens] for part in range(2))
                dve.wait_ge(hi_ready, SPLIT[e] + 1)
                of = bg(e)[:, 0:hi.shape[1] * hi.shape[2]].rearrange("p (k n) -> p k n", n=hi.shape[2])
                emptied(dve.tensor_tensor(lo, of, hi.bitcast(f32), ALU.subtract), e)

            for e in ORDER:
                what, b = e[0], e[1]
                if what == "cT":
                    if b >= 1:
                        dve.wait_ge(bg_full, full(("V", b - 1)))
                    else:
                        angles_in_turns()
                    lo_part(e, cT)
                elif what == "xT":
                    if b >= 1:
                        dve.wait_ge(bg_full, full(("Q", b - 1)))
                    lo_part(e, xnT)
                    if b == 0:
                        taken(dve, ("K", b))
                        stack_rows(dve, link, 0, b)
                elif what[:2] == "aT":
                    t = int(what[2])
                    if b >= 1:
                        bg_read(dve, (f"W{t}", b - 1))
                    lo_part(e, attnT, slice(t * P, (t + 1) * P))
                elif what[:3] == "x2T":
                    t = int(what[3])
                    if b >= 1:
                        bg_read(dve, ("E1", b - 1), ("up3", b - 1))
                    lo_part(e, x2nT, slice(t * P, (t + 1) * P))
                elif what == "ln1a":
                    dve.wait_ge(ld_x[b], 16)
                    if b >= 1:
                        dve.wait_ge(rstd_ready, b)
                    mean_variance(x_sb[:, b * T:(b + 1) * T, :], stats, mv, mv_ready)
                    if b == 0:
                        rotary_angles()
                elif what == "K":
                    if b == 0:
                        rotary_tables()
                    rotate(e, 0, b)
                elif what == "ln1b":
                    dve.wait_ge(rstd_ready, b + 1)
                    if b >= 1:
                        by_token_read(e)
                    normalise(xn, x_sb[:, b * T:(b + 1) * T, :], mv, rstd, xn_ready)
                elif what == "Q":
                    rotate(e, 1, b)
                    if b == 0:
                        taken(dve, e)
                        stack_rows(dve, link, 1, b)
                elif what == "S":
                    n, k = e[1], e[2]
                    m, t, half = n // 2, k // 2, k % 2
                    if k == 0 and n % 2 == 0 and m >= 2:
                        dve.wait_ge(mnat_ready, m - 1)
                        dve.wait_ge(bg_full, full(("MT", m - 2)))
                    dve.wait_ge(s_full, 4 * n + k + 1)
                    dve.tensor_reduce(mneg[m % 2][:, t, n % 2, 2 * half:2 * half + 2],
                                      ps_s[(4 * n + k) % NS][:].rearrange("p (i k) -> p i k", i=2),
                                      AX.X, ALU.max, negate=True).then_inc(s_free, 1)
                    if n % 2 and k == 3:
                        dve.wait_ge(s_free, 4 * (n + 1))
                        of = mneg[m % 2][:].rearrange("p t s i -> p t (s i)")
                        hi, lo = (mnat[m % 2][:, :, part, :] for part in range(2))
                        link(dve.tensor_copy(hi.bitcast(f32r), of))
                        dve.tensor_tensor(lo.bitcast(f32r), of, hi, ALU.subtract).then_inc(mnat_ready, 1)
                elif what[0] == "o":
                    t = int(what[1])
                    dve.wait_ge(bg_full, full(e))
                    by_token_read(e)
                    if b >= 1:
                        taken(dve, (what, b - 1))
                    o = bg(e)[:].rearrange("p (m i s r) -> p m i s r", i=HG, s=2, r=2 * HD)
                    r = rden[:, t, :].rearrange("p (s m i) -> p s m i", s=2, i=HG)
                    for s in range(2):
                        ins = dve.reciprocal(r[:, s, :, :], o[:, :, :, s, HD])
                    link(ins)
                    for s in range(2):
                        to = attn[:, t, :, :].rearrange("p (m s i) d -> p m s i d", s=2, i=HG)[:, :, s, :, :]
                        ins = dve.tensor_tensor(to, o[:, :, :, s, 0:HD],
                                                r[:, s, :, :].unsqueeze(3).broadcast_to((P, G // 2, HG, HD)), ALU.mult)
                    emptied(ins, e)
                elif what[0] == "W":
                    t = int(what[1])
                    dve.wait_ge(bg_full, full(e))
                    dve.wait_ge(xb_ready, b + 1)
                    xv = x_sb[:, b * T + t, :]
                    emptied(dve.tensor_tensor(xv, bg(e)[:, 0:D], xv, ALU.add), e)
                elif what[:4] == "ln2a":
                    t = int(what[4])
                    tile = slice(t, t + 1)
                    taken(dve, (f"W{t}", b))
                    if b >= 1:
                        dve.wait_ge(rstd2_ready, T * (b - 1) + t + 1)
                    mean_variance(x_sb[:, b * T + t:b * T + t + 1, :], stats2[:, tile, :], mv2[:, tile, :], mv2_ready)
                elif what[:4] == "ln2b":
                    t = int(what[4])
                    tile = slice(t, t + 1)
                    dve.wait_ge(rstd2_ready, T * b + t + 1)
                    by_token_read(e)
                    normalise(x2n[:, tile, :], x_sb[:, b * T + t:b * T + t + 1, :], mv2[:, tile, :], rstd2[:, tile],
                              x2n_ready)
                elif what[0] == "E":
                    t = int(what[1])
                    dve.wait_ge(bg_full, full(e))
                    if b >= 1:
                        taken(dve, (what, b - 1))
                    link(dve.max(top8[:, t, :], bg(e)[:, D:D + E]))
                    dve.tensor_tensor(route[:, t:t + 1], top8[:, t, 0:1], top8[:, t, 1:2], ALU.add)\
                        .then_inc(route_ready, 1)
                elif what[:2] == "up" and b == B - 1:
                    squares(dve, e, int(what[2]))
                elif what[0] == "h" and b == B - 1:
                    lo_squares(dve, b, int(what[1]))
                elif what[:4] == "ln3a":
                    t = int(what[4])
                    tile = slice(t, t + 1)
                    dve.wait_ge(dn_full, b + 1)
                    taken(dve, (f"E{t}", b))
                    if b >= 1:
                        dve.wait_ge(fin_ready, T * (b - 1) + t + 1)
                    else:
                        dve.wait_ge(weights_split, WS)
                    dve.tensor_tensor(y[:, t, :], ps_dn[:, t * D:(t + 1) * D], moe[:, t, :], ALU.add).then_inc(y_ready, 1)
                    dve.wait_ge(y_ready, T * b + t + 1)
                    if b >= 1:
                        dve.wait_ge(rstd3_ready, T * (b - 1) + t + 1)
                    mean_variance(y[:, tile, :], stats3[:, tile, :], mv3[:, tile, :], mv3_ready)
                    dve.wait_ge(mv3_ready, T * b + t + 1)
                    dve.scalar_tensor_tensor(out=y[:, t, :], in0=y[:, t, :], scalar=mv3[:, t, 0:1], in1=gamma_sb[:],
                                             op0=ALU.subtract, op1=ALU.mult).then_inc(yn_ready, 1)
                elif what[:4] == "ln3b":
                    t = int(what[4])
                    dve.wait_ge(yn_ready, T * b + t + 1)
                    dve.wait_ge(rstd3_ready, T * b + t + 1)
                    dve.wait_ge(x2b_ready, b + 1)
                    if b >= 1:
                        dve.wait_ge(out_done[t], 16 * b)
                    dve.scalar_tensor_tensor(out=fin[:, t, :], in0=y[:, t, :], scalar=rstd3[:, t:t + 1],
                                             in1=x_sb[:, b * T + t, :], op0=ALU.mult, op1=ALU.add).then_inc(fin_ready, 1)

        @block.tensor
        def _(pe):
            def begin(e):
                k = TURN[e]
                if k >= 2:
                    pe.wait_ge(bg_free[k % 2], k // 2)

            def transposes(e, blocks):
                begin(e)
                at = 0
                for block_ in blocks:
                    m = block_.shape[0]
                    ins = pe.transpose(bg(e)[0:block_.shape[1], at:at + m], block_, ident[:])
                    at += m
                ins.then_inc(bg_full, 1)

            def split_product(to, lhs, rhs, fresh):
                of, in_rhs = fresh
                early, late = (((0, 0), (1, 0)), (0, 1)) if in_rhs else (((0, 0), (0, 1)), (1, 0))
                terms = [(k, a, b_) for k in range(len(lhs)) for a, b_ in early]
                terms += [(k, *late) for k in range(len(lhs))]
                for c, (k, a, b_) in enumerate(terms):
                    if c == 0:
                        pe.wait_ge(hi_ready, SPLIT[of] + 1)
                    if (a, b_) == late and k == 0:
                        taken(pe, of)
                    ins = pe.matmul(to, lhs[k][a], rhs[k][b_], start=(c == 0), stop=(c == len(terms) - 1))
                return ins

            def split_by_token(e, lhs, rhs, kc, cols, fresh):
                begin(e)
                for t in range(T):
                    ins = split_product(bg(e)[:, t * D:(t + 1) * D],
                                        [[lhs[:, a, k, t * P:(t + 1) * P] for a in range(2)] for k in range(kc)],
                                        [[rhs[:, a, k, cols] for a in range(2)] for k in range(kc)], (fresh, False))
                ins.then_inc(bg_full, 1)

            def keep_warm(count):
                for _ in range(count):
                    pe.transpose(ps_st[NST - 1][:, 0:P], ident[:], ident[:])

            pe.wait_ge(ident_ready, 1)
            for e in ORDER:
                what, b = e[0], e[1]
                if b == 0 and what in WARM:
                    keep_warm(WARM[what])
                if b == B - 1 and what in WARM_LAST:
                    keep_warm(WARM_LAST[what])
                if what == "cT":
                    pe.wait_ge(ld_c[b], 16)
                    transposes(e, [c_sb[:, b % 2 * T + t, :] for t in range(T)])
                elif what == "K":
                    if b == 0:
                        pe.wait_ge(raw_lo, 1)
                    split_by_token(e, cT, wkv, 1, slice(0, D), ("cT", b))
                elif what == "V":
                    split_by_token(e, cT, wkv, 1, slice(D, 2 * D), ("cT", b))
                elif what == "xT":
                    pe.wait_ge(xn_ready, b + 1)
                    transposes(e, [xn[:, t, k * P:(k + 1) * P] for k in range(KC) for t in range(T)])
                elif what == "Q":
                    if b == 0:
                        pe.wait_ge(raw_lo, 2)
                    split_by_token(e, xnT, wq, KC, slice(0, D), ("xT", b))
                elif what[:2] in ("ks", "qs"):
                    which, j = int(what[0] == "q"), int(what[2])
                    if b == 0 and j == 0:
                        pe.wait_ge(nat_const, 3)
                    if j == 0:
                        pe.wait_ge(nat_ready[which], b + 1)
                        if b == 0:
                            pe.wait_ge(second_hi, which + 1)
                    rows = nat[which][:].rearrange("p t (g i) r -> p t g (i r)", g=G)
                    transposes(e, [rows[:, t, g, :] for g in (2 * j, 2 * j + 1) for t in range(T)])
                elif what == "S":
                    n, k = e[1], e[2]
                    b, g = step(n)
                    t, half = k // 2, k % 2
                    if g % 2 == 0 and k == 0:
                        if sent(g // 2, b):
                            pe.wait_ge(kmask_ready[g // 2], sent(g // 2, b))
                        else:
                            taken(pe, ("ks0", b))
                        taken(pe, (f"qs{g // 2}", b))
                    if 4 * n + k >= NS:
                        pe.wait_ge(s_free, 4 * n + k - NS + 1)
                    pe.matmul(ps_s[(4 * n + k) % NS][:], qstack[b % 2][:, g, t * P:(t + 1) * P],
                              kmask[:, g, 2 * half:2 * half + 2, :], start=True, stop=True).then_inc(s_full, 1)
                elif what == "MT":
                    m = e[1]
                    pe.wait_ge(mnat_ready, m + 1)
                    transposes(e, [mnat[m % 2][:, t, :, :].rearrange("p a i -> p (a i)") for t in range(T)])
                elif what == "ST":
                    n, i = e[1], e[2]
                    b, g = step(n)
                    k = HG * n + i
                    if i == 0 and n % 2 == 0:
                        pe.wait_ge(m_sent[n // 2 % 2], 64 * (n // 4 + 1))
                    if k >= NST:
                        pe.wait_ge(st_free, k - NST + 1)
                    for t in range(T):
                        ins = pe.matmul(ps_st[k % NST][:, t * N:(t + 1) * N], kmask[:, g, i, t * P:(t + 1) * P],
                                        qstack[b % 2][:, g, :], start=True, stop=True)
                    ins.then_inc(st_full, 1)
                elif what == "PV":
                    n = e[1]
                    b, g = step(n)
                    pe.wait_ge(st_free, HG * (n + 1))
                    if n >= 2 and n % 2 == 0:
                        pe.wait_ge(oT_ready, n // 2)
                    if g == 0:
                        taken(pe, ("V", b))
                    odd = n % 2 == 1
                    for t in range(T):
                        for i in range(HG):
                            ins = pe.matmul(ps_o[Q * i:Q * (i + 1), 0:N],
                                            vaug[b % 2][:, t, HG * (g // 2) + i, 2 * HD * odd:2 * HD * odd + Q],
                                            probs[n % 2][:, i, t, :],
                                            start=(not odd and t == 0), stop=(odd and t == T - 1))
                    ins.then_inc(pv_done, 1)
                elif what[0] == "o":
                    t = int(what[1])
                    pe.wait_ge(oT_ready, G // 2 * (b + 1))
                    transposes(e, [oT[:, m, t * P:(t + 1) * P] for m in range(G // 2)])
                elif what[:2] == "aT":
                    t = int(what[2])
                    taken(pe, (f"o{t}", b))
                    rows = attn.rearrange("p t h d -> p t (h d)")
                    transposes(e, [rows[:, t, k * P:(k + 1) * P] for k in range(KC)])
                elif what[0] == "W":
                    t = int(what[1])
                    if b == 0:
                        pe.wait_ge(weights_split, WS)
                    begin(e)
                    split_product(bg(e)[:, 0:D],
                                  [[attnT[:, a, k, t * P:(t + 1) * P] for a in range(2)] for k in range(KC)],
                                  [[wout[:, a, k, :] for a in range(2)] for k in range(KC)],
                                  ((f"aT{t}", b), False)).then_inc(bg_full, 1)
                elif what[:3] == "x2T":
                    t = int(what[3])
                    pe.wait_ge(x2n_ready, T * b + t + 1)
                    transposes(e, [x2n[:, t, k * P:(k + 1) * P] for k in range(KC)])
                elif what[0] == "E":
                    t = int(what[1])
                    begin(e)
                    split_product(bg(e)[:, 0:D + E],
                                  [[x2nT[:, a, k, t * P:(t + 1) * P] for a in range(2)] for k in range(KC)],
                                  [[expert[:, a, k, :] for a in range(2)] for k in range(KC)],
                                  ((f"x2T{t}", b), False)).then_inc(bg_full, 1)
                elif what[:2] == "up":
                    j = int(what[2])
                    begin(e)
                    for f in range(2):
                        tile = slice((2 * j + f) * P, (2 * j + f + 1) * P)
                        ins = split_product(bg(e)[:, f * N:(f + 1) * N],
                                            [[up[:, a, k, tile] for a in range(2)] for k in range(KC)],
                                            [[x2nT[:, a, k, :] for a in range(2)] for k in range(KC)],
                                            (("x2T1", b), True))
                    ins.then_inc(bg_full, 1)
                elif what[:2] == "dn":
                    j = int(what[2])
                    pe.wait_ge(h_ready, 4 * b + j + 1)
                    if b == 0 and j == 0:
                        pe.wait_ge(down_split, 4)
                    if b >= 1 and j == 0:
                        pe.wait_ge(y_ready, T * b)
                    for t in range(T):
                        terms = [(f, a, c) for f in range(2) for a, c in ((0, 0), (0, 1), (1, 0))]
                        for i, (f, a, c) in enumerate(terms):
                            ins = pe.matmul(ps_dn[:, t * D:(t + 1) * D], inner[:, j % 2, a, f, t * P:(t + 1) * P],
                                            down[:, c, 2 * j + f, :],
                                            start=(j == 0 and t == 0 and i == 0),
                                            stop=(j == 3 and t == T - 1 and i == len(terms) - 1))
                    ins.then_inc(dn_full if j == 3 else dn_read, 1)


_INS = ["x", "ctx_1024", "fside_BxSx2_0", "L0_xattn_Wq", "L0_xattn_Wkv", "L0_xattn_Wout", "L0_xattn_bout",
        "L0_ffn_gate_w", "L0_ffn_up_w", "L0_ffn_down_w", "L0_ffn_expert_weight", "L0_ffn_ln_gamma",
        "L0_ffn_ln_beta"]


def kernel(**inputs):
    import numpy as _np
    import concourse.bacc as _bacc
    from concourse import mybir as _mybir
    from concourse.bass_utils import run_bass_kernel_spmd as _run

    nc = _bacc.Bacc("TRN2", target_bir_lowering=False, num_devices=1)
    arrays, args = {}, []
    for name in _INS:
        a = _np.ascontiguousarray(inputs[name])
        arrays[f"in_{name}"] = a
        args.append(nc.dram_tensor(f"in_{name}", a.shape, _mybir.dt.from_np(a.dtype), kind="ExternalInput").ap())
    result = nc.dram_tensor("result", inputs["x"].shape, _mybir.dt.float32, kind="ExternalOutput").ap()
    xattn_ffn_kernel(nc, *args, result)
    r = _run(nc, [arrays], core_ids=[0])
    return r.results[0]["result"]
```
